# Optimizing a Trainium2 kernel written in Bass

```python
import numpy as np
import jax
import jax.numpy as jnp

def _softmax(x, axis=-1):
    return jax.nn.softmax(x, axis=axis)

def _gelu(x):
    return jax.nn.gelu(x, approximate=True)

def _silu(x):
    return jax.nn.silu(x)

def _sigmoid(x):
    return jax.nn.sigmoid(x)

def _layernorm(x, axis=-1, eps=1e-05):
    m = jnp.mean(x, axis=axis, keepdims=True)
    v = jnp.var(x, axis=axis, keepdims=True)
    return (x - m) / jnp.sqrt(v + eps)

def _scatter_add(tgt, idx, src, axis=0):
    return tgt.at[idx].add(src)

def _segment_sum(src, seg, n):
    return jax.ops.segment_sum(src, seg, n)
kernel_name = 'mk_adj_resnorm_d2_adj_r2_8957dd'

def setup_inputs(seed: int=0):
    np.random.seed(seed)
    _w = jnp.asarray

    def _rec_inputs():
        import jax
        import jax.numpy as jnp
        _gk = jax.random.key(seed)
        x = -0.0004776 + 1.001 * jax.random.normal(jax.random.fold_in(_gk, 1), (1354, 512), jnp.float32)
        _w = (1.0 + jnp.arange(1354, dtype=jnp.float32)) ** (-0.5)
        _w = _w / _w.mean()
        _pij = jnp.clip(0.0014771 * _w[:, None] * _w[None, :], 0.0, 1.0)
        _a = jax.random.uniform(jax.random.fold_in(_gk, 2), (1354, 1354)) < _pij
        _a = jnp.logical_or(_a, jnp.eye(1354, dtype=bool))
        _af = _a.astype(jnp.float32)
        adj = _af
        return (x, adj)
    x, adj = _rec_inputs()

    def _L0_gnn_setup():
        import jax, jax.numpy as jnp
        import numpy as np
        N, H, E, HEADS = (1500, 512, 10000, 8)
        DK = H // HEADS
        key = jax.random.key(seed)
        k1, k2, k3, k4 = jax.random.split(key, 4)
        inst_feature = jax.random.normal(k1, (N, H), dtype=jnp.float32)
        rel_pair_index = jax.random.randint(k2, (E, 2), 0, N, dtype=jnp.int64)
        agg = jnp.zeros((N, N), dtype=jnp.float32)
        agg = agg.at[rel_pair_index[:, 0], rel_pair_index[:, 1]].set(1.0)
        agg = agg.at[jnp.arange(N), jnp.arange(N)].set(1.0)
        std = float(np.sqrt(2.0 / (H + DK)))
        Wq = jax.random.normal(k3, (H, H), dtype=jnp.float32) * std
        Wk = jax.random.normal(k4, (H, H), dtype=jnp.float32) * std
        bq = jnp.zeros((H,), dtype=jnp.float32)
        bk = jnp.zeros((H,), dtype=jnp.float32)
        return {'inst_feature': inst_feature, 'aggregator_matrix': agg, 'rel_pair_index': rel_pair_index, 'Wq': Wq, 'bq': bq, 'Wk': Wk, 'bk': bk}
    _L0_gnn_all = _L0_gnn_setup()
    _L0_gnn_in = {k: v for k, v in _L0_gnn_all.items() if k in ('rel_pair_index', 'Wq', 'bq', 'Wk', 'bk')}
    del _L0_gnn_all

    def _L1_gnn_setup():
        import jax, jax.numpy as jnp
        import numpy as np
        N = 4096
        D_IN = 512
        D_OUT = 512
        key = jax.random.key(seed)
        k1, k2, k3, k4 = jax.random.split(key, 4)
        features = jax.random.normal(k1, (N, D_IN), dtype=jnp.float32)
        adj = jax.random.uniform(k2, (N, N), dtype=jnp.float32)
        W = jax.random.normal(k3, (D_OUT, D_IN), dtype=jnp.float32) * (1.0 / np.sqrt(D_IN))
        b = jax.random.normal(k4, (D_OUT,), dtype=jnp.float32) * 0.01
        return {'features': features, 'adj': adj, 'W': W, 'b': b}
    _L1_gnn_all = _L1_gnn_setup()
    _L1_gnn_in = {k: v for k, v in _L1_gnn_all.items() if k in ('W', 'b')}
    del _L1_gnn_all
    return {'x': x, 'adj': adj, 'L0_gnn_rel_pair_index': _L0_gnn_in['rel_pair_index'], 'L0_gnn_Wq': _L0_gnn_in['Wq'], 'L0_gnn_bq': _L0_gnn_in['bq'], 'L0_gnn_Wk': _L0_gnn_in['Wk'], 'L0_gnn_bk': _L0_gnn_in['bk'], 'L1_gnn_W': _L1_gnn_in['W'], 'L1_gnn_b': _L1_gnn_in['b']}

def reference(x, adj, L0_gnn_rel_pair_index, L0_gnn_Wq, L0_gnn_bq, L0_gnn_Wk, L0_gnn_bk, L1_gnn_W, L1_gnn_b):
    import jax
    import jax.numpy as jnp

    def _L0_gnn_ref(inst_feature, aggregator_matrix, rel_pair_index, Wq, bq, Wk, bk):
        import jax, jax.numpy as jnp
        import numpy as np
        N, H, E, HEADS = (1500, 512, 10000, 8)
        DK = H // HEADS
        n = inst_feature.shape[0]
        sub = rel_pair_index[:, 0]
        obj = rel_pair_index[:, 1]
        q = (inst_feature[sub] @ Wq.T + bq).reshape(-1, HEADS, DK)
        k = (inst_feature[obj] @ Wk.T + bk).reshape(-1, HEADS, DK)
        att = ((q * k).sum(-1) / np.sqrt(DK)).T.astype(inst_feature.dtype)
        scores = jnp.zeros((HEADS, n, n), dtype=inst_feature.dtype)
        scores = scores.at[:, sub, obj].set(att)
        mask = (1.0 - aggregator_matrix).astype(bool)
        scores = jnp.where(mask[None], -jnp.inf, scores)
        di = jnp.arange(n)
        scores = scores.at[:, di, di].set(1e-07)
        attn = jax.nn.softmax(scores, axis=2)
        aggregator_factor = attn.sum(axis=0) / HEADS
        return aggregator_factor @ inst_feature

    def _L1_gnn_ref(features, adj, W, b):
        import jax, jax.numpy as jnp
        import numpy as np
        N = 4096
        D_IN = 512
        D_OUT = 512
        agg = adj @ features
        out = jnp.einsum('nd,od->no', agg, W) + b
        return jax.nn.relu(out)
    x = _layernorm(x + _L0_gnn_ref(x, adj, L0_gnn_rel_pair_index, L0_gnn_Wq, L0_gnn_bq, L0_gnn_Wk, L0_gnn_bk), axis=-1)
    x = _layernorm(x + _L1_gnn_ref(x, adj, L1_gnn_W, L1_gnn_b), axis=-1)
    return x

_drawn_inputs = setup_inputs


def setup_inputs(seed=0):
    import zlib

    import numpy as np

    out = dict(_drawn_inputs(seed))
    spreads = {'L0_gnn_bq': (0.0, 2.0), 'L0_gnn_bk': (0.0, 2.0)}
    factors = {'L0_gnn_Wq': 96.706, 'L0_gnn_Wk': 200.0, 'L1_gnn_b': 8.0}
    for name, (base, spread) in spreads.items():
        noise = np.random.default_rng([zlib.crc32(name.encode()), seed]).standard_normal(out[name].shape)
        drawn = base * np.exp(spread * noise) if base else spread * noise
        out[name] = jnp.asarray(drawn.astype(out[name].dtype))
    for name, factor in factors.items():
        out[name] = (out[name] * factor).astype(out[name].dtype)
    return out
```

```python
import numpy as np
import concourse.bass as bass
from concourse import mybir
from contextlib import ExitStack

F32 = mybir.dt.float32
F16 = mybir.dt.float16
I32 = mybir.dt.int32
ALU = mybir.AluOpType
ACT = mybir.ActivationFunctionType
AX = mybir.AxisListType

N = 1354
D = 512
E = 10000
HEADS = 8
DK = D // HEADS
P = 128
DT = D // P
KT = -(-N // P)
KREM = N - (KT - 1) * P
EP, EC = 125, 80
assert EP * EC == E
EPS = 1e-5
DIAG = 1e-7
BIG = 3e38

GT = 11
GS = (N - P) // (GT - 1) + 1
GP = N - (GT - 1) * GS
assert GP <= P and GP >= GS
CHUNKS = [(c, min(512, N - c)) for c in range(0, N, 512)]


def krows(k):
    return P if k < KT - 1 else KREM


class Steps:

    def __init__(self, sem):
        self.sem, self.base, self.n = sem, 0, 0

    def did(self, ins):
        self.n += 1
        ins.then_inc(self.sem, 1)

    def wait(self, eng):
        eng.wait_ge(self.sem, self.base + self.n)


def general_path(nc, flag, flag_ready, x, xT, adj, adjT, pairs, wqT, bq, wkT, bk, wT, b, x2d, out):
    ctx = ExitStack()
    with ctx:
        def sb(name, shape, dt=F32):
            return ctx.enter_context(nc.sbuf_tensor("g_" + name, shape, dt))

        def sem(name):
            return ctx.enter_context(nc.semaphore("g_" + name))

        xT_sb = sb("xT", [P, DT, N])
        x_sb = sb("x", [P, KT, D])
        w1_sb = sb("w1", [P, DT, D])
        w2_sb = sb("w2", [P, DT, D])
        kh = sb("kh", [DK, HEADS, N])
        qh = sb("qh", [DK, HEADS, GP])
        bqk = sb("bqk", [DK, 2, HEADS])
        brow = sb("brow", [1, D])
        ones_row = sb("ones_row", [1, P])
        pair_i = sb("pair_i", [EP, 2 * EC], I32)
        pair_f = sb("pair_f", [EP, 2, EC])
        neg = sb("neg", [EP, 2, EC])
        one_sub = sb("one_sub", [EP, EC, GP], F16)
        one_obj = sb("one_obj", [EP, 2, N], F16)
        zero16 = sb("zero16", [EP, GP], F16)
        zeroN = sb("zeroN", [EP, 512], F16)
        iota16 = sb("iota16", [P, N], F16)
        col_row = sb("col_row", [GP, N])
        ident = sb("ident", [P, P])
        a_t = sb("a_t", [GP, N])
        on_diag = sb("on_diag", [GP, N])
        edge = sb("edge", [GP, N])
        s_t = sb("s_t", [GP, N])
        p_t = sb("p_t", [GP, N])
        f_t = sb("f_t", [GP, N])
        fT = sb("fT", [P, KT, GP])
        xt = sb("xt", [GP, D])
        z_t = sb("z_t", [GP, D])
        y_t = sb("y_t", [GP, D])
        st = sb("st", [GP, 6])
        mv = sb("mv", [GP, 2])
        sm = sb("sm", [GP, 8])
        token = sb("token", [1, 16])
        agg = a_t[:, 0:D]
        aggT = on_diag
        aT = xT_sb
        psum = ctx.enter_context(nc.psum_tensor("g_psum", [P, 8, 512], F32))
        pflat = psum[:, :, :].rearrange("p b n -> p (b n)")
        even, odd = pflat[:, 0:N], pflat[:, 1536:1536 + N]

        loaded = sem("loaded")
        consts = sem("consts")
        pool_chain = sem("pool_chain")
        kproj = sem("kproj")
        kproj_used = sem("kproj_used")
        tile_in = sem("tile_in")
        q_bias = sem("q_bias")
        q_ps = sem("q_ps")
        q_sb = sem("q_sb")
        sub_ready = sem("sub_ready")
        obj_ready = sem("obj_ready")
        obj_free = sem("obj_free")
        em_ps = sem("em_ps")
        em_used = sem("em_used")
        s_ps = sem("s_ps")
        s_used = sem("s_used")
        s_ok = sem("s_ok")
        p_ok = sem("p_ok")
        f_ok = sem("f_ok")
        fT_ps = sem("fT_ps")
        fT_sb = sem("fT_sb")
        o_ps = sem("o_ps")
        z_ok = sem("z_ok")
        var_ok = sem("var_ok")
        std_ok = sem("std_ok")
        y_ok = sem("y_ok")
        y_out = sem("y_out")
        chain = sem("chain")
        x2_in = sem("x2_in")
        t2_in = sem("t2_in")
        agg_ps = sem("agg_ps")
        agg_sb = sem("agg_sb")
        aggT_ps = sem("aggT_ps")
        aggT_sb = sem("aggT_sb")
        out_ps = sem("out_ps")
        relu_ok = sem("relu_ok")
        z2_ok = sem("z2_ok")
        var2_ok = sem("var2_ok")
        std2_ok = sem("std2_ok")
        y2_ok = sem("y2_ok")
        y2_out = sem("y2_out")
        chain2 = sem("chain2")

        LOADS = 10
        block = ctx.enter_context(nc.Block())

        def flagged(eng):
            if flag is None:
                return None
            eng.wait_ge(flag_ready, 1)
            return eng.value_load(flag[0:1, 0:1], min_val=0, max_val=1)

        @block.sync
        def _(sp):
            def body():
                def load(dst, src):
                    sp.dma_start(dst, src).then_inc(loaded, 16)

                load(xT_sb[:, :, :], xT.rearrange("(t p) n -> p t n", p=P))
                load(w1_sb[:, :, :], wkT.rearrange("(t p) n -> p t n", p=P))
                load(w2_sb[:, :, :], wqT.rearrange("(t p) n -> p t n", p=P))
                load(x_sb[:, 0:KT - 1, :], x[0:(KT - 1) * P, :].rearrange("(t p) n -> p t n", p=P))
                load(x_sb[0:KREM, KT - 1, :], x[(KT - 1) * P:N, :])
                load(pair_i[:, :], pairs.rearrange("(p c) t -> p (c t)", p=EP))
                load(brow[0:1, :], b.rearrange("(o n) -> o n", o=1))
                with nc.allow_non_contiguous_dma(reason="two small bias vectors"):
                    load(bqk[:, 0, :], bq.rearrange("(h d) -> d h", d=DK))
                    load(bqk[:, 1, :], bk.rearrange("(h d) -> d h", d=DK))
                load(xt[0:1, :], x[0:1, :])
                sp.wait_ge(loaded, 16 * LOADS)
                with sp.Fori(0, GT) as i:
                    row = sp.snap(i * GS)
                    sp.wait_ge(y_ok, i + 1)
                    sp.dma_start(a_t[:, :], adj[bass.ds(row, GP), :]).then_inc(tile_in, 16)
                    sp.dma_start(xt[:, :], x[bass.ds(row, GP), :]).then_inc(tile_in, 16)
                    sp.wait_ge(y_ok, i + 2)
                    sp.dma_start(x2d[bass.ds(row, GP), :], y_t[:, :]).then_inc(y_out, 16)
                sp.wait_ge(y_out, 16 * GT + 16)
                sp.dma_start(x_sb[:, 0:KT - 1, :],
                             x2d[0:(KT - 1) * P, :].rearrange("(t p) n -> p t n", p=P)).then_inc(x2_in, 16)
                sp.dma_start(x_sb[0:KREM, KT - 1, :], x2d[(KT - 1) * P:N, :]).then_inc(x2_in, 16)
                sp.dma_start(w1_sb[:, :, :], wT.rearrange("(t p) n -> p t n", p=P)).then_inc(x2_in, 16)
                with sp.Fori(0, GT) as i:
                    row = sp.snap(i * GS)
                    sp.wait_ge(y2_ok, i + 1)
                    aTv = aT.rearrange("p t n -> p (t n)")
                    aTv = aTv[:, 0:KT * GP].rearrange("p (t n) -> p t n", n=GP)
                    sp.dma_start(aTv[:, 0:KT - 1, :],
                                 adjT[0:(KT - 1) * P, bass.ds(row, GP)]
                                 .rearrange("(t p) n -> p t n", p=P)).then_inc(t2_in, 16)
                    sp.dma_start(aTv[0:KREM, KT - 1, :],
                                 adjT[(KT - 1) * P:N, bass.ds(row, GP)]).then_inc(t2_in, 16)
                    sp.dma_start(xt[:, :], x2d[bass.ds(row, GP), :]).then_inc(t2_in, 16)
                    sp.wait_ge(y2_ok, i + 2)
                    sp.dma_start(out[bass.ds(row, GP), :], y_t[:, :]).then_inc(y2_out, 16)
                sp.wait_ge(y2_out, 16 * GT + 16)

            v = flagged(sp)
            if v is None:
                body()
            else:
                with sp.If(v != 0):
                    body()

        @block.gpsimd
        def _(pool):
            def body():
                nc.gpsimd.iota(iota16[:, :], [[1, N]], base=0, channel_multiplier=0,
                               allow_small_or_imprecise_dtypes=True).then_inc(consts, 1)
                nc.gpsimd.iota(col_row[:, :], [[1, N]], base=0, channel_multiplier=-1,
                               allow_small_or_imprecise_dtypes=True).then_inc(consts, 1)
                nc.gpsimd.memset(ident[:, :], 0.0).then_inc(pool_chain, 1)
                nc.gpsimd.memset(zero16[:, :], 0.0).then_inc(consts, 1)
                nc.gpsimd.memset(zeroN[:, :], 0.0).then_inc(consts, 1)
                nc.gpsimd.memset(ones_row[:, :], 1.0).then_inc(consts, 1)
                pool.wait_ge(pool_chain, 1)
                nc.gpsimd.affine_select(out=ident[:, :], in_=ident[:, :], compare_op=ALU.not_equal, fill=1.0,
                                        base=0, pattern=[[-1, P]], channel_multiplier=1).then_inc(consts, 1)

            v = flagged(pool)
            if v is None:
                body()
            else:
                with pool.If(v != 0):
                    body()

        @block.tensor
        def _(pe):
            def body():
                pe.wait_ge(loaded, 16 * LOADS)
                pe.wait_ge(consts, 6)
                n = 0
                for h in range(HEADS):
                    for c, w in CHUNKS:
                        if n >= 2:
                            pe.wait_ge(kproj_used, n - 1)
                        for k in range(DT):
                            last = nc.tensor.matmul(psum[0:DK, n % 2, 0:w], w1_sb[:, k, h * DK:(h + 1) * DK],
                                                    xT_sb[:, k, c:c + w], start=(k == 0), stop=(k == DT - 1))
                        last.then_inc(kproj, 1)
                        n += 1
                pe.wait_ge(kproj_used, n)
                with pe.Fori(0, GT) as i:
                    for h in range(HEADS):
                        for k in range(DT):
                            last = nc.tensor.matmul(psum[0:DK, 6 + h // 4, (h % 4) * GP:(h % 4 + 1) * GP],
                                                    w2_sb[:, k, h * DK:(h + 1) * DK],
                                                    xT_sb[:, k, bass.ds(i * GS, GP)],
                                                    start=(k == 0), stop=(k == DT - 1))
                    last.then_inc(q_ps, 1)
                    pe.wait_ge(z_ok, i + 1)
                    pe.wait_ge(sub_ready, i + 1)
                    for c, w in CHUNKS:
                        nc.tensor.matmul(even[0:GP, c:c + w], zero16[:, :], zeroN[:, 0:w], start=True, stop=False)
                    with pe.Fori(0, EC // 2) as c2:
                        for u in range(2):
                            pe.wait_ge(obj_ready, i * EC + c2 * 2 + (u + 1))
                            for c, w in CHUNKS:
                                last = nc.tensor.matmul(even[0:GP, c:c + w], one_sub[:, bass.ds(c2 * 2 + u, 1), :].rearrange("p o n -> p (o n)"),
                                                        one_obj[:, u, c:c + w], start=False, stop=False)
                            last.then_inc(obj_free, 1)
                    for c, w in CHUNKS:
                        last = nc.tensor.matmul(even[0:GP, c:c + w], zero16[:, :], zeroN[:, 0:w], start=False, stop=True)
                    last.then_inc(em_ps, 1)
                    pe.wait_ge(q_sb, i + 1)
                    for h in range(HEADS):
                        if h == 0:
                            pe.wait_ge(em_used, i + 1)
                        elif h == 1:
                            pe.wait_ge(fT_sb, 4 * i + 4)
                        else:
                            pe.wait_ge(s_used, i * HEADS + (HEADS + h - 1))
                        s_bank = even if h % 2 == 0 else odd
                        for c, w in CHUNKS:
                            last = nc.tensor.matmul(s_bank[0:GP, c:c + w], qh[:, h, :], kh[:, h, c:c + w],
                                                    start=True, stop=True)
                        last.then_inc(s_ps, 1)
                    pe.wait_ge(f_ok, i + 1)
                    for k in range(KT):
                        r = krows(k)
                        last = nc.tensor.transpose(psum[0:r, 3 + k // 4, (k % 4) * P:(k % 4) * P + GP],
                                                   f_t[:, k * P:k * P + r], ident[0:GP, 0:GP])
                    last.then_inc(fT_ps, 1)
                    pe.wait_ge(fT_sb, 4 * i + 8)
                    for k in range(KT):
                        r = krows(k)
                        last = nc.tensor.matmul(psum[0:GP, 0, :], fT[0:r, k, :], x_sb[0:r, k, :],
                                                start=(k == 0), stop=(k == KT - 1))
                    last.then_inc(o_ps, 1)
                pe.wait_ge(z_ok, GT + 1)
                pe.wait_ge(x2_in, 48)
                with pe.Fori(0, GT) as i:
                    aTv = aT.rearrange("p t n -> p (t n)")
                    aTv = aTv[:, 0:KT * GP].rearrange("p (t n) -> p t n", n=GP)
                    pe.wait_ge(t2_in, 48 * i + 48)
                    for k in range(KT):
                        r = krows(k)
                        last = nc.tensor.matmul(psum[0:GP, 0, :], aTv[0:r, k, :], x_sb[0:r, k, :],
                                                start=(k == 0), stop=(k == KT - 1))
                    last.then_inc(agg_ps, 1)
                    pe.wait_ge(agg_sb, i + 1)
                    for k in range(DT):
                        last = nc.tensor.transpose(psum[:, 1, k * P:k * P + GP], agg[:, k * P:(k + 1) * P],
                                                   ident[0:GP, 0:GP])
                    last.then_inc(aggT_ps, 1)
                    pe.wait_ge(aggT_sb, i + 1)
                    nc.tensor.matmul(psum[0:GP, 2, :], ones_row[0:1, 0:GP], brow[0:1, :], start=True, stop=False)
                    for k in range(DT):
                        last = nc.tensor.matmul(psum[0:GP, 2, :], fT[:, k, :], w1_sb[:, k, :],
                                                start=False, stop=(k == DT - 1))
                    last.then_inc(out_ps, 1)

            v = flagged(pe)
            if v is None:
                body()
            else:
                with pe.If(v != 0):
                    body()

        @block.scalar
        def _(act):
            def body():
                act.wait_ge(loaded, 16 * LOADS)
                n = 0
                for h in range(HEADS):
                    for c, w in CHUNKS:
                        act.wait_ge(kproj, n + 1)
                        nc.scalar.activation(kh[:, h, c:c + w], psum[0:DK, n % 2, 0:w], ACT.Identity,
                                             bias=bqk[:, 1, h:h + 1]).then_inc(kproj_used, 1)
                        n += 1
                with act.Fori(0, GT) as i:
                    act.wait_ge(q_ps, i + 1)
                    act.wait_ge(q_bias, 1)
                    act.wait_ge(s_used, i * HEADS + HEADS)
                    for h in range(HEADS):
                        last = nc.scalar.activation(qh[:, h, :], psum[0:DK, 6 + h // 4, (h % 4) * GP:(h % 4 + 1) * GP],
                                                    ACT.Identity, bias=bqk[:, 0, h:h + 1], scale=DK ** -0.5)
                    last.then_inc(q_sb, 1)
                    for h in range(HEADS):
                        act.wait_ge(s_ok, i * HEADS + (h + 1))
                        nc.scalar.activation(p_t[:, :], s_t[:, :], ACT.Exp, bias=sm[:, 0:1],
                                             accum_out=sm[:, 1:2]).then_inc(p_ok, 1)
                    act.wait_ge(fT_ps, i + 1)
                    for g in range(3):
                        w = 4 if g < 2 else 2
                        src = psum[:, 3 + g, 0:w * P].rearrange("p (t n) -> p t n", n=P)[:, :, 0:GP]
                        nc.scalar.activation(fT[:, 4 * g:4 * g + w, :], src, ACT.Copy).then_inc(fT_sb, 1)
                    nc.scalar.activation(fT[0:KREM, KT - 1, :], psum[0:KREM, 5, 2 * P:2 * P + GP],
                                         ACT.Copy).then_inc(fT_sb, 1)
                    act.wait_ge(var_ok, i + 1)
                    nc.scalar.activation(sm[:, 5:6], sm[:, 4:5], ACT.Sqrt).then_inc(std_ok, 1)
                with act.Fori(0, GT) as i:
                    act.wait_ge(agg_ps, i + 1)
                    nc.scalar.activation(agg, psum[0:GP, 0, :], ACT.Copy).then_inc(agg_sb, 1)
                    act.wait_ge(aggT_ps, i + 1)
                    act.wait_ge(out_ps, i + 1)
                    src = psum[:, 1, :].rearrange("p (t n) -> p t n", n=P)[:, :, 0:GP]
                    nc.scalar.activation(fT[:, 0:DT, :], src, ACT.Copy).then_inc(aggT_sb, 1)
                    act.wait_ge(out_ps, i + 2)
                    act.wait_ge(y2_out, 16 * i + 16)
                    nc.scalar.activation(z_t[:, :], psum[0:GP, 2, :], ACT.Relu).then_inc(relu_ok, 1)
                    act.wait_ge(var2_ok, i + 1)
                    nc.scalar.activation(sm[:, 5:6], sm[:, 4:5], ACT.Sqrt).then_inc(std2_ok, 1)

            v = flagged(act)
            if v is None:
                body()
            else:
                with act.If(v != 0):
                    body()

        @block.vector
        def _(dve):
            def body():
                step = Steps(chain)

                def link(ins):
                    step.did(ins)
                    step.wait(dve)

                dve.wait_ge(loaded, 16 * LOADS)
                dve.wait_ge(consts, 6)
                nc.vector.tensor_scalar(bqk[:, 0, :], bqk[:, 0, :], DK ** -0.5, None, ALU.mult).then_inc(q_bias, 1)
                link(nc.vector.tensor_copy(pair_f[:, :, :], pair_i[:, :].rearrange("p (c t) -> p t c", t=2)))
                link(nc.vector.tensor_scalar(neg[:, :, :], pair_f[:, :, :], 0.0, float(N), ALU.is_lt, ALU.mult))
                link(nc.vector.tensor_tensor(pair_f[:, :, :], pair_f[:, :, :], neg[:, :, :], ALU.add))
                starts = ((obj_free, 2), (y_ok, 1), (z_ok, 1), (s_used, HEADS), (fT_sb, 4),
                          (y_out, 16), (y2_ok, 1), (out_ps, 1), (y2_out, 16))
                for n, (free, count) in enumerate(starts):
                    nc.vector.memset(token[:, n:n + 1], 0.0).then_inc(free, count)
                before = step.n
                with dve.Fori(0, GT) as i:
                    step.base, step.n = i * PER1, before
                    nc.vector.tensor_tensor(one_sub[:, :, :],
                                            pair_f[:, 0, :].unsqueeze(2).to_broadcast([EP, EC, GP]),
                                            iota16[0:EP, None, 0:GP].to_broadcast([EP, EC, GP]),
                                            ALU.is_equal).then_inc(sub_ready, 1)
                    with dve.Fori(0, EC // 2) as c2:
                        for u in range(2):
                            dve.wait_ge(obj_free, i * EC + c2 * 2 + (u + 1))
                            nc.vector.tensor_scalar(one_obj[:, u, :], iota16[0:EP, :],
                                                    pair_f[:, 1, bass.ds(c2 * 2 + u, 1)], None,
                                                    ALU.is_equal).then_inc(obj_ready, 1)
                    dve.wait_ge(tile_in, 32 * i + 32)
                    link(nc.vector.tensor_scalar(on_diag[:, :], col_row[:, :], 0.0, None, ALU.is_equal))
                    link(nc.vector.tensor_scalar(col_row[:, :], col_row[:, :], -float(GS), None, ALU.add))
                    link(nc.vector.tensor_scalar(a_t[:, :], a_t[:, :], 1.0, None, ALU.is_equal))
                    link(nc.vector.tensor_tensor(a_t[:, :], a_t[:, :], on_diag[:, :], ALU.max))
                    link(nc.vector.tensor_scalar(a_t[:, :], a_t[:, :], -1.0, BIG, ALU.add, ALU.mult))
                    link(nc.vector.scalar_tensor_tensor(a_t[:, :], on_diag[:, :], DIAG, a_t[:, :],
                                                        ALU.mult, ALU.add))
                    dve.wait_ge(em_ps, i + 1)
                    step.did(nc.vector.tensor_scalar(edge[:, :], even[0:GP, :], 1.0, None, ALU.min))
                    step.wait(dve)
                    nc.vector.scalar_tensor_tensor(edge[:, :], on_diag[:, :], 0.5, edge[:, :],
                                                   ALU.is_lt, ALU.mult).then_inc(em_used, 1)
                    dve.wait_ge(em_used, i + 1)
                    for h in range(HEADS):
                        s_bank = even if h % 2 == 0 else odd
                        dve.wait_ge(s_ps, i * HEADS + (h + 1))
                        nc.vector.tensor_tensor(s_t[:, :], s_bank[0:GP, :], edge[:, :], ALU.mult).then_inc(s_used, 1)
                        dve.wait_ge(s_used, i * HEADS + (HEADS + h + 1))
                        link(nc.vector.tensor_tensor(s_t[:, :], s_t[:, :], a_t[:, :], ALU.add))
                        nc.vector.tensor_reduce(sm[:, 0:1], s_t[:, :], AX.X, ALU.max, negate=True).then_inc(s_ok, 1)
                        dve.wait_ge(p_ok, i * HEADS + (h + 1))
                        link(nc.vector.reciprocal(sm[:, 2:3], sm[:, 1:2]))
                        if h == 0:
                            ins = nc.vector.tensor_scalar(f_t[:, :], p_t[:, :], sm[:, 2:3], None, ALU.mult)
                        else:
                            ins = nc.vector.scalar_tensor_tensor(f_t[:, :], p_t[:, :], sm[:, 2:3], f_t[:, :],
                                                                 ALU.mult, ALU.add)
                        link(ins)
                    nc.vector.tensor_scalar(pair_f[:, 0, :], pair_f[:, 0, :], -float(GS), None,
                                            ALU.add).then_inc(f_ok, 1)
                    dve.wait_ge(f_ok, i + 1)
                    dve.wait_ge(o_ps, i + 1)
                    nc.vector.scalar_tensor_tensor(z_t[:, :], psum[0:GP, 0, :], 1.0 / HEADS, xt[:, :],
                                                   ALU.mult, ALU.add).then_inc(z_ok, 1)
                    dve.wait_ge(z_ok, i + 2)
                    link(nc.vector.bn_stats(st[:, :], z_t[:, :]))
                    nc.vector.tensor_copy(sm[:, 7:8], st[:, 0:1])
                    link(nc.vector.bn_aggr(mv[:, :], st[:, :]))
                    nc.vector.tensor_scalar(sm[:, 4:5], mv[:, 1:2], EPS, None, ALU.add).then_inc(var_ok, 1)
                    dve.wait_ge(std_ok, i + 1)
                    link(nc.vector.reciprocal(sm[:, 6:7], sm[:, 5:6]))
                    dve.wait_ge(y_out, 16 * i + 16)
                    nc.vector.tensor_scalar(y_t[:, :], z_t[:, :], mv[:, 0:1], sm[:, 6:7],
                                            ALU.subtract, ALU.mult).then_inc(y_ok, 1)
                    assert step.n - before == PER1, step.n - before
                step = Steps(chain2)
                with dve.Fori(0, GT) as i:
                    step.base, step.n = i * PER2, 0
                    dve.wait_ge(t2_in, 48 * i + 48)
                    dve.wait_ge(relu_ok, i + 1)
                    nc.vector.tensor_tensor(z_t[:, :], z_t[:, :], xt[:, :], ALU.add).then_inc(z2_ok, 1)
                    dve.wait_ge(z2_ok, i + 1)
                    step.did(nc.vector.bn_stats(st[:, :], z_t[:, :]))
                    step.wait(dve)
                    nc.vector.tensor_copy(sm[:, 7:8], st[:, 0:1])
                    step.did(nc.vector.bn_aggr(mv[:, :], st[:, :]))
                    step.wait(dve)
                    nc.vector.tensor_scalar(sm[:, 4:5], mv[:, 1:2], EPS, None, ALU.add).then_inc(var2_ok, 1)
                    dve.wait_ge(std2_ok, i + 1)
                    step.did(nc.vector.reciprocal(sm[:, 6:7], sm[:, 5:6]))
                    step.wait(dve)
                    dve.wait_ge(y2_out, 16 * i + 16)
                    nc.vector.tensor_scalar(y_t[:, :], z_t[:, :], mv[:, 0:1], sm[:, 6:7],
                                            ALU.subtract, ALU.mult).then_inc(y2_ok, 1)
                    assert step.n == PER2, step.n

            v = flagged(dve)
            if v is None:
                body()
            else:
                with dve.If(v != 0):
                    body()


PER1 = 7 + 3 * HEADS + 3
PER2 = 3


def build(nc, x, adj, pairs, wq, bq, wk, bk, w, b, xT, adjT, wqT, wkT, wT, x2d, out):
    general_path(nc, None, None, x, xT, adj, adjT, pairs, wqT, bq, wkT, bk, wT, b, x2d, out)


def kernel(**inputs):
    import numpy as _np
    import concourse.bacc as _bacc
    from concourse import mybir as _mybir
    from concourse.bass_utils import run_bass_kernel_spmd as _run

    nc = _bacc.Bacc("TRN2", target_bir_lowering=False, num_devices=1)
    given = {
        "x": inputs["x"], "adj": inputs["adj"], "pairs": inputs["L0_gnn_rel_pair_index"],
        "bq": inputs["L0_gnn_bq"], "bk": inputs["L0_gnn_bk"], "b": inputs["L1_gnn_b"],
        "xT": _np.asarray(inputs["x"]).T, "adjT": _np.asarray(inputs["adj"]).T,
        "wqT": _np.asarray(inputs["L0_gnn_Wq"]).T, "wkT": _np.asarray(inputs["L0_gnn_Wk"]).T,
        "wT": _np.asarray(inputs["L1_gnn_W"]).T,
    }
    arrays, aps = {}, {}
    for name, a in given.items():
        a = _np.ascontiguousarray(a)
        arrays["in_" + name] = a
        aps[name] = nc.dram_tensor("in_" + name, a.shape, _mybir.dt.from_np(a.dtype), kind="ExternalInput").ap()
    out = nc.dram_tensor("out", (N, D), F32, kind="ExternalOutput").ap()
    x2d = nc.dram_tensor("x2d", (N, D), F32, kind="Internal").ap()
    build(nc, aps["x"], aps["adj"], aps["pairs"], None, aps["bq"], None, aps["bk"], None, aps["b"],
          aps["xT"], aps["adjT"], aps["wqT"], aps["wkT"], aps["wT"], x2d, out)
    r = _run(nc, [arrays], core_ids=[0])
    return r.results[0]["out"]
```

```python
import numpy as np
import concourse.bass as bass
from concourse import mybir
from contextlib import ExitStack

F32 = mybir.dt.float32
F16 = mybir.dt.float16
I32 = mybir.dt.int32
ALU = mybir.AluOpType
ACT = mybir.ActivationFunctionType
AX = mybir.AxisListType

N = 1354
D = 512
E = 10000
HEADS = 8
DK = D // HEADS
P = 128
DT = D // P
KT = -(-N // P)
KREM = N - (KT - 1) * P
EP, EC = 125, 80
assert EP * EC == E
EPS = 1e-5
DIAG = 1e-7
BIG = 3e38

GT = 11
GS = (N - P) // (GT - 1) + 1
GP = N - (GT - 1) * GS
assert GP <= P and GP >= GS
CHUNKS = [(c, min(512, N - c)) for c in range(0, N, 512)]


STAGES = 4
HALF = 64
SLOTS = HALF - 1
XS = 1024.0
AS = 32.0
WS = 256.0
YS = AS * WS
ALPHA = float(np.exp(np.float32(-DIAG)))
ALPHA1 = float(-np.expm1(-DIAG))
X_SQ_MAX = 3600.0
W_SQ_MAX = 5e4
DEG_MAX = 90.0
V_SQ_MAX = 3e9
G1 = 6


def krows(k):
    return P if k < KT - 1 else KREM


class Steps:

    def __init__(self, sem):
        self.sem, self.base, self.n = sem, 0, 0

    def did(self, ins):
        self.n += 1
        ins.then_inc(self.sem, 1)

    def wait(self, eng):
        eng.wait_ge(self.sem, self.base + self.n)


def general_path(nc, flag, flag_ready, x, xT, adj, adjT, pairs, wqT, bq, wkT, bk, wT, b, x2d, out):
    ctx = ExitStack()
    with ctx:
        def sb(name, shape, dt=F32):
            return ctx.enter_context(nc.sbuf_tensor("g_" + name, shape, dt))

        def sem(name):
            return ctx.enter_context(nc.semaphore("g_" + name))

        xT_sb = sb("xT", [P, DT, N])
        x_sb = sb("x", [P, KT, D])
        w1_sb = sb("w1", [P, DT, D])
        w2_sb = sb("w2", [P, DT, D])
        kh = sb("kh", [DK, HEADS, N])
        qh = sb("qh", [DK, HEADS, GP])
        bqk = sb("bqk", [DK, 2, HEADS])
        brow = sb("brow", [1, D])
        ones_row = sb("ones_row", [1, P])
        pair_i = sb("pair_i", [EP, 2 * EC], I32)
        pair_f = sb("pair_f", [EP, 2, EC])
        neg = sb("neg", [EP, 2, EC])
        one_sub = sb("one_sub", [EP, EC, GP], F16)
        one_obj = sb("one_obj", [EP, 2, N], F16)
        zero16 = sb("zero16", [EP, GP], F16)
        zeroN = sb("zeroN", [EP, 512], F16)
        iota16 = sb("iota16", [P, N], F16)
        col_row = sb("col_row", [GP, N])
        ident = sb("ident", [P, P])
        a_t = sb("a_t", [GP, N])
        on_diag = sb("on_diag", [GP, N])
        edge = sb("edge", [GP, N])
        s_t = sb("s_t", [GP, N])
        p_t = sb("p_t", [GP, N])
        f_t = sb("f_t", [GP, N])
        fT = sb("fT", [P, KT, GP])
        xt = sb("xt", [GP, D])
        z_t = sb("z_t", [GP, D])
        y_t = sb("y_t", [GP, D])
        st = sb("st", [GP, 6])
        mv = sb("mv", [GP, 2])
        sm = sb("sm", [GP, 8])
        token = sb("token", [1, 16])
        agg = a_t[:, 0:D]
        aggT = on_diag
        aT = xT_sb
        psum = ctx.enter_context(nc.psum_tensor("g_psum", [P, 8, 512], F32))
        pflat = psum[:, :, :].rearrange("p b n -> p (b n)")
        even, odd = pflat[:, 0:N], pflat[:, 1536:1536 + N]

        loaded = sem("loaded")
        consts = sem("consts")
        pool_chain = sem("pool_chain")
        kproj = sem("kproj")
        kproj_used = sem("kproj_used")
        tile_in = sem("tile_in")
        q_bias = sem("q_bias")
        q_ps = sem("q_ps")
        q_sb = sem("q_sb")
        sub_ready = sem("sub_ready")
        obj_ready = sem("obj_ready")
        obj_free = sem("obj_free")
        em_ps = sem("em_ps")
        em_used = sem("em_used")
        s_ps = sem("s_ps")
        s_used = sem("s_used")
        s_ok = sem("s_ok")
        p_ok = sem("p_ok")
        f_ok = sem("f_ok")
        fT_ps = sem("fT_ps")
        fT_sb = sem("fT_sb")
        o_ps = sem("o_ps")
        z_ok = sem("z_ok")
        var_ok = sem("var_ok")
        std_ok = sem("std_ok")
        y_ok = sem("y_ok")
        y_out = sem("y_out")
        chain = sem("chain")
        x2_in = sem("x2_in")
        t2_in = sem("t2_in")
        agg_ps = sem("agg_ps")
        agg_sb = sem("agg_sb")
        aggT_ps = sem("aggT_ps")
        aggT_sb = sem("aggT_sb")
        out_ps = sem("out_ps")
        relu_ok = sem("relu_ok")
        z2_ok = sem("z2_ok")
        var2_ok = sem("var2_ok")
        std2_ok = sem("std2_ok")
        y2_ok = sem("y2_ok")
        y2_out = sem("y2_out")
        chain2 = sem("chain2")

        LOADS = 10
        block = ctx.enter_context(nc.Block())

        def flagged(eng):
            if flag is None:
                return None
            if flag_ready is not None:
                eng.wait_ge(flag_ready, 1)
            return eng.value_load(flag[0:1, 0:1], min_val=0, max_val=1)

        @block.sync
        def _(sp):
            def body():
                def load(dst, src):
                    sp.dma_start(dst, src).then_inc(loaded, 16)

                load(xT_sb[:, :, :], xT.rearrange("(t p) n -> p t n", p=P))
                load(w1_sb[:, :, :], wkT.rearrange("(t p) n -> p t n", p=P))
                load(w2_sb[:, :, :], wqT.rearrange("(t p) n -> p t n", p=P))
                load(x_sb[:, 0:KT - 1, :], x[0:(KT - 1) * P, :].rearrange("(t p) n -> p t n", p=P))
                load(x_sb[0:KREM, KT - 1, :], x[(KT - 1) * P:N, :])
                load(pair_i[:, :], pairs.rearrange("(p c) t -> p (c t)", p=EP))
                load(brow[0:1, :], b.rearrange("(o n) -> o n", o=1))
                with nc.allow_non_contiguous_dma(reason="two small bias vectors"):
                    load(bqk[:, 0, :], bq.rearrange("(h d) -> d h", d=DK))
                    load(bqk[:, 1, :], bk.rearrange("(h d) -> d h", d=DK))
                load(xt[0:1, :], x[0:1, :])
                sp.wait_ge(loaded, 16 * LOADS)
                with sp.Fori(0, GT) as i:
                    row = sp.snap(i * GS)
                    sp.wait_ge(y_ok, i + 1)
                    sp.dma_start(a_t[:, :], adj[bass.ds(row, GP), :]).then_inc(tile_in, 16)
                    sp.dma_start(xt[:, :], x[bass.ds(row, GP), :]).then_inc(tile_in, 16)
                    sp.wait_ge(y_ok, i + 2)
                    sp.dma_start(x2d[bass.ds(row, GP), :], y_t[:, :]).then_inc(y_out, 16)
                sp.wait_ge(y_out, 16 * GT + 16)
                sp.dma_start(x_sb[:, 0:KT - 1, :],
                             x2d[0:(KT - 1) * P, :].rearrange("(t p) n -> p t n", p=P)).then_inc(x2_in, 16)
                sp.dma_start(x_sb[0:KREM, KT - 1, :], x2d[(KT - 1) * P:N, :]).then_inc(x2_in, 16)
                sp.dma_start(w1_sb[:, :, :], wT.rearrange("(t p) n -> p t n", p=P)).then_inc(x2_in, 16)
                with sp.Fori(0, GT) as i:
                    row = sp.snap(i * GS)
                    sp.wait_ge(y2_ok, i + 1)
                    aTv = aT.rearrange("p t n -> p (t n)")
                    aTv = aTv[:, 0:KT * GP].rearrange("p (t n) -> p t n", n=GP)
                    sp.dma_start(aTv[:, 0:KT - 1, :],
                                 adjT[0:(KT - 1) * P, bass.ds(row, GP)]
                                 .rearrange("(t p) n -> p t n", p=P)).then_inc(t2_in, 16)
                    sp.dma_start(aTv[0:KREM, KT - 1, :],
                                 adjT[(KT - 1) * P:N, bass.ds(row, GP)]).then_inc(t2_in, 16)
                    sp.dma_start(xt[:, :], x2d[bass.ds(row, GP), :]).then_inc(t2_in, 16)
                    sp.wait_ge(y2_ok, i + 2)
                    sp.dma_start(out[bass.ds(row, GP), :], y_t[:, :]).then_inc(y2_out, 16)
                sp.wait_ge(y2_out, 16 * GT + 16)

            v = flagged(sp)
            if v is None:
                body()
            else:
                with sp.If(v != 0):
                    body()

        @block.gpsimd
        def _(pool):
            def body():
                nc.gpsimd.iota(iota16[:, :], [[1, N]], base=0, channel_multiplier=0,
                               allow_small_or_imprecise_dtypes=True).then_inc(consts, 1)
                nc.gpsimd.iota(col_row[:, :], [[1, N]], base=0, channel_multiplier=-1,
                               allow_small_or_imprecise_dtypes=True).then_inc(consts, 1)
                nc.gpsimd.memset(ident[:, :], 0.0).then_inc(pool_chain, 1)
                nc.gpsimd.memset(zero16[:, :], 0.0).then_inc(consts, 1)
                nc.gpsimd.memset(zeroN[:, :], 0.0).then_inc(consts, 1)
                nc.gpsimd.memset(ones_row[:, :], 1.0).then_inc(consts, 1)
                pool.wait_ge(pool_chain, 1)
                nc.gpsimd.affine_select(out=ident[:, :], in_=ident[:, :], compare_op=ALU.not_equal, fill=1.0,
                                        base=0, pattern=[[-1, P]], channel_multiplier=1).then_inc(consts, 1)

            v = flagged(pool)
            if v is None:
                body()
            else:
                with pool.If(v != 0):
                    body()

        @block.tensor
        def _(pe):
            def body():
                pe.wait_ge(loaded, 16 * LOADS)
                pe.wait_ge(consts, 6)
                n = 0
                for h in range(HEADS):
                    for c, w in CHUNKS:
                        if n >= 2:
                            pe.wait_ge(kproj_used, n - 1)
                        for k in range(DT):
                            last = nc.tensor.matmul(psum[0:DK, n % 2, 0:w], w1_sb[:, k, h * DK:(h + 1) * DK],
                                                    xT_sb[:, k, c:c + w], start=(k == 0), stop=(k == DT - 1))
                        last.then_inc(kproj, 1)
                        n += 1
                pe.wait_ge(kproj_used, n)
                with pe.Fori(0, GT) as i:
                    for h in range(HEADS):
                        for k in range(DT):
                            last = nc.tensor.matmul(psum[0:DK, 6 + h // 4, (h % 4) * GP:(h % 4 + 1) * GP],
                                                    w2_sb[:, k, h * DK:(h + 1) * DK],
                                                    xT_sb[:, k, bass.ds(i * GS, GP)],
                                                    start=(k == 0), stop=(k == DT - 1))
                    last.then_inc(q_ps, 1)
                    pe.wait_ge(z_ok, i + 1)
                    pe.wait_ge(sub_ready, i + 1)
                    for c, w in CHUNKS:
                        nc.tensor.matmul(even[0:GP, c:c + w], zero16[:, :], zeroN[:, 0:w], start=True, stop=False)
                    with pe.Fori(0, EC // 2) as c2:
                        for u in range(2):
                            pe.wait_ge(obj_ready, i * EC + c2 * 2 + (u + 1))
                            for c, w in CHUNKS:
                                last = nc.tensor.matmul(even[0:GP, c:c + w], one_sub[:, bass.ds(c2 * 2 + u, 1), :].rearrange("p o n -> p (o n)"),
                                                        one_obj[:, u, c:c + w], start=False, stop=False)
                            last.then_inc(obj_free, 1)
                    for c, w in CHUNKS:
                        last = nc.tensor.matmul(even[0:GP, c:c + w], zero16[:, :], zeroN[:, 0:w], start=False, stop=True)
                    last.then_inc(em_ps, 1)
                    pe.wait_ge(q_sb, i + 1)
                    for h in range(HEADS):
                        if h == 0:
                            pe.wait_ge(em_used, i + 1)
                        elif h == 1:
                            pe.wait_ge(fT_sb, 4 * i + 4)
                        else:
                            pe.wait_ge(s_used, i * HEADS + (HEADS + h - 1))
                        s_bank = even if h % 2 == 0 else odd
                        for c, w in CHUNKS:
                            last = nc.tensor.matmul(s_bank[0:GP, c:c + w], qh[:, h, :], kh[:, h, c:c + w],
                                                    start=True, stop=True)
                        last.then_inc(s_ps, 1)
                    pe.wait_ge(f_ok, i + 1)
                    for k in range(KT):
                        r = krows(k)
                        last = nc.tensor.transpose(psum[0:r, 3 + k // 4, (k % 4) * P:(k % 4) * P + GP],
                                                   f_t[:, k * P:k * P + r], ident[0:GP, 0:GP])
                    last.then_inc(fT_ps, 1)
                    pe.wait_ge(fT_sb, 4 * i + 8)
                    for k in range(KT):
                        r = krows(k)
                        last = nc.tensor.matmul(psum[0:GP, 0, :], fT[0:r, k, :], x_sb[0:r, k, :],
                                                start=(k == 0), stop=(k == KT - 1))
                    last.then_inc(o_ps, 1)
                pe.wait_ge(z_ok, GT + 1)
                pe.wait_ge(x2_in, 48)
                with pe.Fori(0, GT) as i:
                    aTv = aT.rearrange("p t n -> p (t n)")
                    aTv = aTv[:, 0:KT * GP].rearrange("p (t n) -> p t n", n=GP)
                    pe.wait_ge(t2_in, 48 * i + 48)
                    for k in range(KT):
                        r = krows(k)
                        last = nc.tensor.matmul(psum[0:GP, 0, :], aTv[0:r, k, :], x_sb[0:r, k, :],
                                                start=(k == 0), stop=(k == KT - 1))
                    last.then_inc(agg_ps, 1)
                    pe.wait_ge(agg_sb, i + 1)
                    for k in range(DT):
                        last = nc.tensor.transpose(psum[:, 1, k * P:k * P + GP], agg[:, k * P:(k + 1) * P],
                                                   ident[0:GP, 0:GP])
                    last.then_inc(aggT_ps, 1)
                    pe.wait_ge(aggT_sb, i + 1)
                    nc.tensor.matmul(psum[0:GP, 2, :], ones_row[0:1, 0:GP], brow[0:1, :], start=True, stop=False)
                    for k in range(DT):
                        last = nc.tensor.matmul(psum[0:GP, 2, :], fT[:, k, :], w1_sb[:, k, :],
                                                start=False, stop=(k == DT - 1))
                    last.then_inc(out_ps, 1)

            v = flagged(pe)
            if v is None:
                body()
            else:
                with pe.If(v != 0):
                    body()

        @block.scalar
        def _(act):
            def body():
                act.wait_ge(loaded, 16 * LOADS)
                n = 0
                for h in range(HEADS):
                    for c, w in CHUNKS:
                        act.wait_ge(kproj, n + 1)
                        nc.scalar.activation(kh[:, h, c:c + w], psum[0:DK, n % 2, 0:w], ACT.Identity,
                                             bias=bqk[:, 1, h:h + 1]).then_inc(kproj_used, 1)
                        n += 1
                with act.Fori(0, GT) as i:
                    act.wait_ge(q_ps, i + 1)
                    act.wait_ge(q_bias, 1)
                    act.wait_ge(s_used, i * HEADS + HEADS)
                    for h in range(HEADS):
                        last = nc.scalar.activation(qh[:, h, :], psum[0:DK, 6 + h // 4, (h % 4) * GP:(h % 4 + 1) * GP],
                                                    ACT.Identity, bias=bqk[:, 0, h:h + 1], scale=DK ** -0.5)
                    last.then_inc(q_sb, 1)
                    for h in range(HEADS):
                        act.wait_ge(s_ok, i * HEADS + (h + 1))
                        nc.scalar.activation(p_t[:, :], s_t[:, :], ACT.Exp, bias=sm[:, 0:1],
                                             accum_out=sm[:, 1:2]).then_inc(p_ok, 1)
                    act.wait_ge(fT_ps, i + 1)
                    for g in range(3):
                        w = 4 if g < 2 else 2
                        src = psum[:, 3 + g, 0:w * P].rearrange("p (t n) -> p t n", n=P)[:, :, 0:GP]
                        nc.scalar.activation(fT[:, 4 * g:4 * g + w, :], src, ACT.Copy).then_inc(fT_sb, 1)
                    nc.scalar.activation(fT[0:KREM, KT - 1, :], psum[0:KREM, 5, 2 * P:2 * P + GP],
                                         ACT.Copy).then_inc(fT_sb, 1)
                    act.wait_ge(var_ok, i + 1)
                    nc.scalar.activation(sm[:, 5:6], sm[:, 4:5], ACT.Sqrt).then_inc(std_ok, 1)
                with act.Fori(0, GT) as i:
                    act.wait_ge(agg_ps, i + 1)
                    nc.scalar.activation(agg, psum[0:GP, 0, :], ACT.Copy).then_inc(agg_sb, 1)
                    act.wait_ge(aggT_ps, i + 1)
                    act.wait_ge(out_ps, i + 1)
                    src = psum[:, 1, :].rearrange("p (t n) -> p t n", n=P)[:, :, 0:GP]
                    nc.scalar.activation(fT[:, 0:DT, :], src, ACT.Copy).then_inc(aggT_sb, 1)
                    act.wait_ge(out_ps, i + 2)
                    act.wait_ge(y2_out, 16 * i + 16)
                    nc.scalar.activation(z_t[:, :], psum[0:GP, 2, :], ACT.Relu).then_inc(relu_ok, 1)
                    act.wait_ge(var2_ok, i + 1)
                    nc.scalar.activation(sm[:, 5:6], sm[:, 4:5], ACT.Sqrt).then_inc(std2_ok, 1)

            v = flagged(act)
            if v is None:
                body()
            else:
                with act.If(v != 0):
                    body()

        @block.vector
        def _(dve):
            def body():
                step = Steps(chain)

                def link(ins):
                    step.did(ins)
                    step.wait(dve)

                dve.wait_ge(loaded, 16 * LOADS)
                dve.wait_ge(consts, 6)
                nc.vector.tensor_scalar(bqk[:, 0, :], bqk[:, 0, :], DK ** -0.5, None, ALU.mult).then_inc(q_bias, 1)
                link(nc.vector.tensor_copy(pair_f[:, :, :], pair_i[:, :].rearrange("p (c t) -> p t c", t=2)))
                link(nc.vector.tensor_scalar(neg[:, :, :], pair_f[:, :, :], 0.0, float(N), ALU.is_lt, ALU.mult))
                link(nc.vector.tensor_tensor(pair_f[:, :, :], pair_f[:, :, :], neg[:, :, :], ALU.add))
                starts = ((obj_free, 2), (y_ok, 1), (z_ok, 1), (s_used, HEADS), (fT_sb, 4),
                          (y_out, 16), (y2_ok, 1), (out_ps, 1), (y2_out, 16))
                for n, (free, count) in enumerate(starts):
                    nc.vector.memset(token[:, n:n + 1], 0.0).then_inc(free, count)
                before = step.n
                with dve.Fori(0, GT) as i:
                    step.base, step.n = i * PER1, before
                    nc.vector.tensor_tensor(one_sub[:, :, :],
                                            pair_f[:, 0, :].unsqueeze(2).to_broadcast([EP, EC, GP]),
                                            iota16[0:EP, None, 0:GP].to_broadcast([EP, EC, GP]),
                                            ALU.is_equal).then_inc(sub_ready, 1)
                    with dve.Fori(0, EC // 2) as c2:
                        for u in range(2):
                            dve.wait_ge(obj_free, i * EC + c2 * 2 + (u + 1))
                            nc.vector.tensor_scalar(one_obj[:, u, :], iota16[0:EP, :],
                                                    pair_f[:, 1, bass.ds(c2 * 2 + u, 1)], None,
                                                    ALU.is_equal).then_inc(obj_ready, 1)
                    dve.wait_ge(tile_in, 32 * i + 32)
                    link(nc.vector.tensor_scalar(on_diag[:, :], col_row[:, :], 0.0, None, ALU.is_equal))
                    link(nc.vector.tensor_scalar(col_row[:, :], col_row[:, :], -float(GS), None, ALU.add))
                    link(nc.vector.tensor_scalar(a_t[:, :], a_t[:, :], 1.0, None, ALU.is_equal))
                    link(nc.vector.tensor_tensor(a_t[:, :], a_t[:, :], on_diag[:, :], ALU.max))
                    link(nc.vector.tensor_scalar(a_t[:, :], a_t[:, :], -1.0, BIG, ALU.add, ALU.mult))
                    link(nc.vector.scalar_tensor_tensor(a_t[:, :], on_diag[:, :], DIAG, a_t[:, :],
                                                        ALU.mult, ALU.add))
                    dve.wait_ge(em_ps, i + 1)
                    step.did(nc.vector.tensor_scalar(edge[:, :], even[0:GP, :], 1.0, None, ALU.min))
                    step.wait(dve)
                    nc.vector.scalar_tensor_tensor(edge[:, :], on_diag[:, :], 0.5, edge[:, :],
                                                   ALU.is_lt, ALU.mult).then_inc(em_used, 1)
                    dve.wait_ge(em_used, i + 1)
                    for h in range(HEADS):
                        s_bank = even if h % 2 == 0 else odd
                        dve.wait_ge(s_ps, i * HEADS + (h + 1))
                        nc.vector.tensor_tensor(s_t[:, :], s_bank[0:GP, :], edge[:, :], ALU.mult).then_inc(s_used, 1)
                        dve.wait_ge(s_used, i * HEADS + (HEADS + h + 1))
                        link(nc.vector.tensor_tensor(s_t[:, :], s_t[:, :], a_t[:, :], ALU.add))
                        nc.vector.tensor_reduce(sm[:, 0:1], s_t[:, :], AX.X, ALU.max, negate=True).then_inc(s_ok, 1)
                        dve.wait_ge(p_ok, i * HEADS + (h + 1))
                        link(nc.vector.reciprocal(sm[:, 2:3], sm[:, 1:2]))
                        if h == 0:
                            ins = nc.vector.tensor_scalar(f_t[:, :], p_t[:, :], sm[:, 2:3], None, ALU.mult)
                        else:
                            ins = nc.vector.scalar_tensor_tensor(f_t[:, :], p_t[:, :], sm[:, 2:3], f_t[:, :],
                                                                 ALU.mult, ALU.add)
                        link(ins)
                    nc.vector.tensor_scalar(pair_f[:, 0, :], pair_f[:, 0, :], -float(GS), None,
                                            ALU.add).then_inc(f_ok, 1)
                    dve.wait_ge(f_ok, i + 1)
                    dve.wait_ge(o_ps, i + 1)
                    nc.vector.scalar_tensor_tensor(z_t[:, :], psum[0:GP, 0, :], 1.0 / HEADS, xt[:, :],
                                                   ALU.mult, ALU.add).then_inc(z_ok, 1)
                    dve.wait_ge(z_ok, i + 2)
                    link(nc.vector.bn_stats(st[:, :], z_t[:, :]))
                    nc.vector.tensor_copy(sm[:, 7:8], st[:, 0:1])
                    link(nc.vector.bn_aggr(mv[:, :], st[:, :]))
                    nc.vector.tensor_scalar(sm[:, 4:5], mv[:, 1:2], EPS, None, ALU.add).then_inc(var_ok, 1)
                    dve.wait_ge(std_ok, i + 1)
                    link(nc.vector.reciprocal(sm[:, 6:7], sm[:, 5:6]))
                    dve.wait_ge(y_out, 16 * i + 16)
                    nc.vector.tensor_scalar(y_t[:, :], z_t[:, :], mv[:, 0:1], sm[:, 6:7],
                                            ALU.subtract, ALU.mult).then_inc(y_ok, 1)
                    assert step.n - before == PER1, step.n - before
                step = Steps(chain2)
                with dve.Fori(0, GT) as i:
                    step.base, step.n = i * PER2, 0
                    dve.wait_ge(t2_in, 48 * i + 48)
                    dve.wait_ge(relu_ok, i + 1)
                    nc.vector.tensor_tensor(z_t[:, :], z_t[:, :], xt[:, :], ALU.add).then_inc(z2_ok, 1)
                    dve.wait_ge(z2_ok, i + 1)
                    step.did(nc.vector.bn_stats(st[:, :], z_t[:, :]))
                    step.wait(dve)
                    nc.vector.tensor_copy(sm[:, 7:8], st[:, 0:1])
                    step.did(nc.vector.bn_aggr(mv[:, :], st[:, :]))
                    step.wait(dve)
                    nc.vector.tensor_scalar(sm[:, 4:5], mv[:, 1:2], EPS, None, ALU.add).then_inc(var2_ok, 1)
                    dve.wait_ge(std2_ok, i + 1)
                    step.did(nc.vector.reciprocal(sm[:, 6:7], sm[:, 5:6]))
                    step.wait(dve)
                    dve.wait_ge(y2_out, 16 * i + 16)
                    nc.vector.tensor_scalar(y_t[:, :], z_t[:, :], mv[:, 0:1], sm[:, 6:7],
                                            ALU.subtract, ALU.mult).then_inc(y2_ok, 1)
                    assert step.n == PER2, step.n

            v = flagged(dve)
            if v is None:
                body()
            else:
                with dve.If(v != 0):
                    body()


PER1 = 7 + 3 * HEADS + 3
PER2 = 3


def fast_path(nc, flag, x, adj, adjT, diag, pairs, wqT, bq, wkT, bk, wT, b, out):
    ctx = ExitStack()
    with ctx:
        def sb(name, shape, dt=F32):
            return ctx.enter_context(nc.sbuf_tensor("f_" + name, shape, dt))

        def sem(name):
            return ctx.enter_context(nc.semaphore("f_" + name))

        stage = sb("stage", [P, STAGES * N])
        adj32 = [stage[:, s * N:(s + 1) * N] for s in range(STAGES)]
        wqk = stage[:, 0:2 * DT * D].rearrange("p (w t n) -> p w t n", w=2, t=DT)
        a16 = sb("a16", [P, KT, N], F16)
        x_agg = sb("x_agg", [P, KT * D])
        x32 = x_agg[:, :].rearrange("p (t n) -> p t n", n=D)
        agg16 = x_agg[:, 0:DT * N].bitcast(F16).rearrange("p (h t n) -> p h t n", h=2, t=DT)
        x16 = sb("x16", [P, 2, KT, D], F16)
        x2 = sb("x2", [P, KT, D])
        late = sb("late", [P, KT * D])
        x216 = late[:, :].bitcast(F16).rearrange("p (h t n) -> p h t n", h=2, n=D)
        w16 = sb("w16", [P, 2, DT, D], F16)
        shared = sb("shared", [P, 2 * N])
        w32 = shared[:, 0:DT * D].rearrange("p (t n) -> p t n", n=D)
        one_slot = shared[0:EP, 0:EC * HALF // 2].bitcast(F16).rearrange("p (c s) -> p c s", s=HALF)
        a_row, a_col = shared[:, 0:N], shared[:, N:2 * N]
        square = sb("square", [P, N])
        tx = sb("tx", [P, 2, D])
        z = sb("z", [P, 3, D])
        st = sb("st", [P, 4, 6])
        mv = sb("mv", [P, 4, 2])
        sd = sb("sd", [P, 4])
        rs = sb("rs", [P, 4])
        deg = sb("deg", [P, KT])
        cb = sb("cb", [P, KT])
        gb = sb("gb", [P, KT])
        rzb = sb("rzb", [P, KT])
        eps26 = sb("eps26", [P, 1])
        eps1 = sb("eps1", [P, 1])
        half = sb("half", [P, 1])
        quarter = sb("quarter", [P, 1])
        one1 = sb("one1", [P, 1])
        epsy = sb("epsy", [P, 1])
        ste = sb("ste", [P, 2, 6])
        mve = sb("mve", [P, 2, 2])
        sde = sb("sde", [P, 2])
        rse = sb("rse", [P, 2])
        adj_off = sb("adj_off", [P, KT])
        x_sq = sb("x_sq", [P, KT])
        seen = sb("seen", [P, 7])
        limit = sb("limit", [P, 7])
        kept = sb("kept", [P, 7])
        kept1 = sb("kept1", [P, 1])
        kept16 = sb("kept16", [P, 1], F16)
        diag_sb = sb("diag_sb", [2, N // 2])
        pair_i = sb("pair_i", [EP, 2 * EC], I32)
        pair_f = sb("pair_f", [EP, 2, EC])
        tmp_e = sb("tmp_e", [EP, 2, EC])
        valid = sb("valid", [EP, EC])
        look_f = sb("look_f", [EP, EC])
        look_i = sb("look_i", [EP, EC], I32)
        looked = sb("looked", [EP, EC])
        vals = sb("vals", [EP, EC, 3], F16)
        active = sb("active", [EP, EC])
        upto = sb("upto", [EP, EC])
        zero_e = sb("zero_e", [EP, EC])
        total16 = sb("total16", [EP, 1], F16)
        pos = sb("pos", [EP, EC])
        pos16 = sb("pos16", [EP, EC], F16)
        cap = sb("cap", [EP, HALF], F16)
        tri = sb("tri", [EP, EP], F16)
        ones16 = sb("ones16", [P, P], F16)
        slot = sb("slot", [P, 3])
        slot_i = sb("slot_i", [P, 2], I32)
        same = sb("same", [P, HALF])
        lower = sb("lower", [P, HALF])
        ident = sb("ident", [P, P])
        ident16 = sb("ident16", [P, P], F16)
        slot16 = sb("slot16", [HALF, 3], F16)
        spread = sb("spread", [HALF, 3, 2, HALF], F16)
        twice16 = sb("twice16", [HALF, 2, HALF], F16)
        across = sb("across", [P, 3, P])
        rowm = sb("rowm", [P, P])
        pairm = sb("pairm", [P, HALF])
        junk = sb("junk", [P, HALF])
        rowoff = sb("rowoff", [P, HALF])
        later = sb("later", [P, 2])
        ul = sb("ul", [P, 2])
        used32 = sb("used32", [P, 1])
        last32 = sb("last32", [P, 1])
        iota16 = sb("iota16", [P, N], F16)
        xs = sb("xs", [P, D])
        xo = sb("xo", [P, D])
        bqk = sb("bqk", [P, 2, DT])
        hsel = sb("hsel", [P, 2, P])
        mx = sb("mx", [P, HEADS])
        arg = sb("arg", [P, 3, HEADS])
        ex = sb("ex", [P, 3, HEADS])
        exu = sb("exu", [P, HEADS + 1])
        nrow = sb("nrow", [P, 1])
        nn = sb("nn", [P, 1])
        zz = sb("zz", [P, HEADS])
        cdw = sb("cdw", [P, 3])
        sm = sb("sm", [P, 8])
        ar16 = sb("ar16", [P, N], F16)
        ac16 = sb("ac16", [P, N], F16)
        bt = sb("bt", [P, D])
        v16 = sb("v16", [P, D], F16)
        psum = ctx.enter_context(nc.psum_tensor("f_psum", [P, 8, 512], F32))

        def at(place, first, *dims):
            size = 1
            for n in dims:
                size *= n
            flat = place[:, first:first + size]
            return flat if len(dims) == 1 else flat.rearrange("p (a b) -> p a b", b=dims[1])

        xsoT = at(late, 0, 8, HALF)
        kb = at(late, 512, DT, HALF)
        qk = at(late, 768, DT, HALF)
        sT = at(late, 1024, HEADS, HALF)
        sI = at(late, 1536, HEADS, HALF)
        txe = at(late, 2048, 2, D)
        ze = at(late, 3072, 2, D)
        xoc = late[0:HALF, 4096:4096 + D]
        arT = at(late, 4608, KT * P // 2).bitcast(F16).rearrange("p (t n) -> p t n", n=P)
        d16 = at(late, 5312, D // 2).bitcast(F16)
        delta = tx[:, 0, :]
        hi_tmp = tx[:, 1, :].bitcast(F16).rearrange("p (a n) -> p a n", n=D)
        dT16 = square[:, 512:1024].bitcast(F16).rearrange("p (h t n) -> p h t n", h=2, n=P)
        vv = z[:, 2, :]
        oh16 = iota16
        y = at(stage, 0, 3, D)

        pairs_in = sem("pairs_in")
        x_in = [sem(f"x_in{k}") for k in range(KT)]
        adj_in = [sem(f"adj_in{s}") for s in range(STAGES)]
        w_in = sem("w_in")
        small_in = sem("small_in")
        bt_in = sem("bt_in")
        wqk_in = sem("wqk_in")
        pool_chain = sem("pool_chain")
        bt_zero = sem("bt_zero")
        looked_in = sem("looked_in")
        xs_in, xo_in = sem("xs_in"), sem("xo_in")
        arow_in, acol_in = sem("arow_in"), sem("acol_in")
        act_chain = sem("act_chain")
        x_hi = sem("x_hi")
        adj_checked = sem("adj_checked")
        tx_ok = sem("tx_ok")
        sd_ok = sem("sd_ok")
        x2_hi = sem("x2_hi")
        agg_hi = sem("agg_hi")
        w_hi = sem("w_hi")
        checks = sem("checks")
        ar_ok = sem("ar_ok")
        xsoT_ok = sem("xsoT_ok")
        kb_ok = sem("kb_ok")
        ex_ok = sem("ex_ok")
        arT_ok = sem("arT_ok")
        txe_ok = sem("txe_ok")
        sde_ok = sem("sde_ok")
        dT_hi = sem("dT_hi")
        vsq_ok = sem("vsq_ok")
        sd2_ok = sem("sd2_ok")
        chain = sem("chain")
        look_ok = sem("look_ok")
        a16_ok = sem("a16_ok")
        x_lo = sem("x_lo")
        w_lo = sem("w_lo")
        z_ok = sem("z_ok")
        var_ok = sem("var_ok")
        x2_ok = sem("x2_ok")
        x2_lo = sem("x2_lo")
        agg_lo = sem("agg_lo")
        coef_ok = sem("coef_ok")
        total_ok = sem("total_ok")
        one_ok = sem("one_ok")
        slot_ok = sem("slot_ok")
        index_ok = sem("index_ok")
        rowm_ok = sem("rowm_ok")
        ac_ok = sem("ac_ok")
        oh_ok = sem("oh_ok")
        qk_ok = sem("qk_ok")
        arg_ok = sem("arg_ok")
        exu_ok = sem("exu_ok")
        coefe_ok = sem("coefe_ok")
        xoc_ok = sem("xoc_ok")
        ze_ok = sem("ze_ok")
        delta_ok = sem("delta_ok")
        d16_ok = sem("d16_ok")
        dT_lo = sem("dT_lo")
        v_ok = sem("v_ok")
        v16_ok = sem("v16_ok")
        kept_ok = sem("kept_ok")
        flag_ok = sem("flag_ok")
        small_ok = sem("small_ok")
        sT_used = sem("sT_used")
        y_used = sem("y_used")
        z2_ok = sem("z2_ok")
        var2_ok = sem("var2_ok")
        y_ok = sem("y_ok")
        l0_ps = sem("l0_ps")
        deg_ps = sem("deg_ps")
        agg_ps = sem("agg_ps")
        off_ps = sem("off_ps")
        slot_ps = sem("slot_ps")
        across_ps = sem("across_ps")
        xsoT_ps = sem("xsoT_ps")
        qk_ps = sem("qk_ps")
        sT_ps = sem("sT_ps")
        arT_ps = sem("arT_ps")
        zz_ps = sem("zz_ps")
        axe_ps = sem("axe_ps")
        corr_ps = sem("corr_ps")
        dT_ps = sem("dT_ps")
        dw_ps = sem("dw_ps")
        kept_ps = sem("kept_ps")
        y_ps = sem("y_ps")
        r_ps = sem("r_ps")
        out_done = [sem(f"out_done{s}") for s in range(3)]

        L0_BANK = [0, 1, 2, 3, 4, 5, 7, 0, 1, 2, 3]
        DEG_BANK = 6
        A_BANK = [4, 5, 6, 7, 0, 1]
        BLOCKS = [(2 * r + d, c) for r in range(2) for c in range(3) for d in range(2)]
        YB = 5
        Y_BANK = [A_BANK[i % YB] for i in range(KT)]
        R_BANK = [2 + i % 2 for i in range(KT)]
        POOL_STEPS = 4 + 2 * 7 + 5

        block = ctx.enter_context(nc.Block())

        @block.sync
        def _(sp):
            sp.dma_start(pair_i[:, :], pairs.rearrange("(p c) t -> p (c t)", p=EP)).then_inc(pairs_in, 16)
            for k in range(KT):
                r = krows(k)
                sp.dma_start(x32[0:r, k, :], x[k * P:k * P + r, :]).then_inc(x_in[k], 16)
                if k >= STAGES:
                    sp.wait_ge(a16_ok, k - STAGES + 1)
                    sp.wait_ge(adj_checked, k - STAGES + 1)
                sp.dma_start(adj32[k % STAGES][0:r, :], adjT[k * P:k * P + r, :]).then_inc(adj_in[k % STAGES], 16)
                if k == 3:
                    sp.dma_start(w32, wT.rearrange("(t p) n -> p t n", p=P)).then_inc(w_in, 16)
                    sp.wait_ge(bt_zero, 1)
                    for s in (SLOTS, HALF + SLOTS):
                        sp.dma_start(bt[s:s + 1, :], b.rearrange("(o n) -> o n", o=1)).then_inc(bt_in, 16)
                    with nc.allow_non_contiguous_dma(reason="small vectors"):
                        sp.dma_start(bqk[:, 0, :], bq.rearrange("(t p) -> p t", p=P)).then_inc(small_in, 16)
                        sp.dma_start(bqk[:, 1, :], bk.rearrange("(t p) -> p t", p=P)).then_inc(small_in, 16)
                    sp.dma_start(diag_sb[:, :], diag.rearrange("(p n) -> p n", p=2)).then_inc(small_in, 16)
            sp.wait_ge(a16_ok, KT)
            sp.wait_ge(adj_checked, KT)
            sp.dma_start(wqk[:, 0, :, :], wqT.rearrange("(t p) n -> p t n", p=P)).then_inc(wqk_in, 16)
            sp.dma_start(wqk[:, 1, :, :], wkT.rearrange("(t p) n -> p t n", p=P)).then_inc(wqk_in, 16)
            for i in range(KT):
                r = krows(i)
                sp.wait_ge(y_ok, i + 1)
                sp.dma_start(out[i * P:i * P + r, :], y[0:r, i % 3, :]).then_inc(out_done[i % 3], 16)
            for s in range(3):
                sp.wait_ge(out_done[s], 16 * len(range(s, KT, 3)))

        @block.gpsimd
        def _(pool):
            g = nc.gpsimd
            did = Steps(pool_chain)

            def diagonal(t, fill):
                return g.affine_select(out=t, in_=t, compare_op=ALU.not_equal, fill=fill, base=0,
                                       pattern=[[-1, t.shape[-1]]], channel_multiplier=1)

            def link(ins):
                did.did(ins)
                did.wait(pool)

            link(g.memset(ones16[:, :], 1.0))
            g.memset(bt[:, :], 0.0).then_inc(bt_zero, 1)
            link(g.memset(ident[:, :], 0.0))
            link(diagonal(ident[:, :], 1.0))
            link(g.tensor_copy(ident16[:, :], ident[:, :]))
            for q in range(2):
                link(g.tensor_copy(same[q * HALF:(q + 1) * HALF, :], ident[q * HALF:(q + 1) * HALF, q * HALF:(q + 1) * HALF]))
                link(g.tensor_copy(twice16[:, q, :], ident[0:HALF, 0:HALF]))
                link(g.memset(lower[q * HALF:(q + 1) * HALF, :], 1.0))
                link(g.affine_select(out=lower[q * HALF:(q + 1) * HALF, :], in_=lower[q * HALF:(q + 1) * HALF, :],
                                     compare_op=ALU.is_gt, fill=0.0, base=0, pattern=[[-1, HALF]],
                                     channel_multiplier=1))
                link(g.tensor_scalar(last32[q * HALF:(q + 1) * HALF, :], same[q * HALF:(q + 1) * HALF, SLOTS:HALF], AS, 0.0, ALU.mult, ALU.add))
                link(g.memset(hsel[q * HALF:(q + 1) * HALF, q, :], DK ** -0.5))
                link(g.memset(hsel[(1 - q) * HALF:(2 - q) * HALF, q, :], 0.0))
            link(g.memset(tri[:, :], 1.0))
            link(g.affine_select(out=tri[:, :], in_=tri[:, :], compare_op=ALU.is_gt, fill=0.0, base=0,
                                 pattern=[[1, EP]], channel_multiplier=-1))
            link(g.iota(iota16[:, :], [[1, N]], base=0, channel_multiplier=0,
                        allow_small_or_imprecise_dtypes=True))
            link(g.iota(cap[:, 0:SLOTS], [[1, SLOTS]], base=1, channel_multiplier=0,
                        allow_small_or_imprecise_dtypes=True))
            link(g.memset(cap[:, SLOTS:HALF], -1.0))
            assert did.n == POOL_STEPS, did.n
            pool.wait_ge(look_ok, 1)
            for c in range(EC):
                g.indirect_dma_start(looked[:, c:c + 1], None,
                                     adj.rearrange("a (b o) -> (a b) o", o=1),
                                     bass.IndirectOffsetOnAxis(look_i[:, c:c + 1], 0)).then_inc(looked_in, 16)
            pool.wait_ge(index_ok, 1)
            pool.wait_ge(slot_ps, 1)

            def rows(dst, src, which, done):
                g.indirect_dma_start(dst, None, src,
                                     bass.IndirectOffsetOnAxis(slot_i[:, which:which + 1], 0)).then_inc(done, 16)

            rows(xs[:, :], x, 0, xs_in)
            rows(xo[:, :], x, 1, xo_in)
            rows(a_row, adj, 0, arow_in)
            rows(a_col, adjT, 0, acol_in)

        @block.scalar
        def _(act):
            s = nc.scalar
            did = Steps(act_chain)

            def link(ins):
                did.did(ins)
                did.wait(act)

            act.wait_ge(small_ok, 1)
            for k in range(KT):
                r = krows(k)
                act.wait_ge(x_in[k], 16)
                s.activation(x16[0:r, 0, k, :], x32[0:r, k, :], ACT.Identity, scale=XS).then_inc(x_hi, 1)
                act.wait_ge(adj_in[k % STAGES], 16 * (k // STAGES + 1))
                if k:
                    act.wait_ge(adj_checked, k)
                link(s.activation(square[0:r, :], adj32[k % STAGES][0:r, :], ACT.Square, bias=half[0:r, :]))
                s.activation(square[0:r, :], square[0:r, :], ACT.Square, bias=quarter[0:r, :],
                             accum_out=adj_off[0:r, k:k + 1]).then_inc(adj_checked, 1)
                if k == 5:
                    act.wait_ge(w_in, 16)
                    s.activation(w16[:, 0, :, :], w32, ACT.Identity, scale=WS).then_inc(w_hi, 1)
            act.wait_ge(coef_ok, 2)

            def share(i):
                r = krows(i)
                if i >= 2:
                    act.wait_ge(z_ok, i - 1)
                s.activation(tx[0:r, i % 2, :], x32[0:r, i, :], ACT.Identity, scale=gb[0:r, i:i + 1]).then_inc(tx_ok, 1)

            def root(i):
                r = krows(i)
                act.wait_ge(var_ok, i + 1)
                s.activation(sd[0:r, i % 4:i % 4 + 1], mv[0:r, i % 4, 1:2], ACT.Sqrt, bias=eps26[0:r, :],
                             scale=1.0 / YS ** 2).then_inc(sd_ok, 1)

            def high(i):
                r = krows(i)
                act.wait_ge(x2_ok, i + 1)
                s.activation(x216[0:r, 0, i, :], x2[0:r, i, :], ACT.Identity, scale=XS / YS).then_inc(x2_hi, 1)

            share(0)
            for i in range(KT):
                if i + 1 < KT:
                    share(i + 1)
                root(i)
                if i >= 1:
                    high(i - 1)
            high(KT - 1)
            act.wait_ge(adj_checked, KT)
            for k in range(KT):
                r = krows(k)
                link(s.activation(square[0:r, 0:D], x32[0:r, k, :], ACT.Square, accum_out=x_sq[0:r, k:k + 1]))
            act.wait_ge(small_in, 48)
            link(s.activation(square[0:2, 0:N // 2], diag_sb[:, :], ACT.Square, bias=one1[0:2, :],
                              accum_out=seen[0:2, 6:7]))
            s.activation(square[:, :].bitcast(F16)[:, 0:DT * D], w16[:, 0, :, :].rearrange("p t n -> p (t n)"),
                         ACT.Square, accum_out=seen[:, 2:3]).then_inc(checks, 1)

            def agg_high(n):
                t, c = BLOCKS[n]
                c0, w = CHUNKS[c]
                act.wait_ge(agg_ps, n + 1)
                if n == 0:
                    did.wait(act)
                s.activation(agg16[:, 0, t, c0:c0 + w], psum[:, A_BANK[n % 6], 0:w], ACT.Identity,
                             scale=AS / XS).then_inc(agg_hi, 1)

            def edge_rows():
                act.wait_ge(arow_in, 16)
                s.activation(ar16[:, :], a_row, ACT.Identity, accum_out=nrow[:, :]).then_inc(ar_ok, 1)

            def edge_xT():
                act.wait_ge(xsoT_ps, 1)
                s.activation(xsoT[:, :, :], psum[:, 3, :].rearrange("p (t n) -> p t n", n=HALF),
                             ACT.Identity).then_inc(xsoT_ok, 1)

            def edge_k():
                act.wait_ge(qk_ps, 1)
                for t in range(DT):
                    last = s.activation(kb[:, t, :], psum[:, 2, 256 + t * HALF:256 + (t + 1) * HALF], ACT.Identity,
                                        bias=bqk[:, 1, t:t + 1])
                last.then_inc(kb_ok, 1)

            def edge_exp():
                act.wait_ge(arg_ok, 1)
                s.activation(ex[:, :, :], arg[:, :, :], ACT.Exp).then_inc(ex_ok, 1)

            def edge_aT():
                act.wait_ge(arT_ps, 1)
                src = psum[:, 2, :].bitcast(F16).rearrange("p (t n) -> p t n", n=P)
                s.activation(arT[:, 0:8, :], src, ACT.Identity).then_inc(arT_ok, 1)
                rest = psum[:, 1, :].bitcast(F16).rearrange("p (t n) -> p t n", n=P)
                s.activation(arT[:, 8:KT - 1, :], rest[:, 0:KT - 9, :], ACT.Identity).then_inc(arT_ok, 1)
                s.activation(arT[0:KREM, KT - 1, :], rest[0:KREM, KT - 9, :], ACT.Identity).then_inc(arT_ok, 1)

            def edge_share():
                act.wait_ge(coefe_ok, 1)
                act.wait_ge(xs_in, 16)
                s.activation(txe[:, 0, :], xs[:, :], ACT.Identity, scale=sm[:, 3:4]).then_inc(txe_ok, 1)
                s.activation(txe[:, 1, :], xs[:, :], ACT.Identity, scale=sm[:, 7:8]).then_inc(txe_ok, 1)

            def edge_root():
                act.wait_ge(ze_ok, 1)
                s.activation(sde[:, :], mve[:, :, 1:2].rearrange("p a o -> p (a o)"), ACT.Sqrt, bias=eps1[:, :],
                             scale=1.0 / XS ** 2).then_inc(sde_ok, 1)

            def edge_dT():
                act.wait_ge(dT_ps, 1)
                s.activation(dT16[:, 0, :, :], psum[:, 3, :].rearrange("p (t n) -> p t n", n=P),
                             ACT.Identity).then_inc(dT_hi, 1)

            def edge_v():
                act.wait_ge(v_ok, 1)
                s.activation(square[:, 0:D], vv[:, :], ACT.Square, accum_out=seen[:, 5:6]).then_inc(vsq_ok, 1)

            def root2(i):
                r = krows(i)
                act.wait_ge(var2_ok, i + 1)
                s.activation(sd[0:r, i % 4:i % 4 + 1], mv[0:r, i % 4, 1:2], ACT.Sqrt, bias=epsy[0:r, :]).then_inc(sd2_ok, 1)

            for n in range(2 * G1):
                agg_high(n)
            edge_rows()
            edge_xT()
            edge_k()
            edge_exp()
            edge_aT()
            edge_share()
            edge_root()
            edge_dT()
            edge_v()
            for i in range(KT):
                root2(i)

        @block.vector
        def _(dve):
            v = nc.vector
            did = Steps(chain)

            def link(ins):
                did.did(ins)
                did.wait(dve)

            for t, value in ((half, -0.5), (quarter, -0.25), (one1, -1.0), (eps26, EPS * (XS / YS) ** 2),
                             (eps1, EPS), (epsy, EPS * YS ** 2), (adj_off, 0.0), (x_sq, 0.0), (seen, 0.0),
                             (deg, 0.0)):
                did.did(v.memset(t[:, :], value))
            for n, top in enumerate((0.0, X_SQ_MAX, W_SQ_MAX * WS ** 2, DEG_MAX, float(SLOTS), V_SQ_MAX, 0.0)):
                did.did(v.memset(limit[:, n:n + 1], top))
            did.did(v.memset(zero_e[:, :], 0.0))
            v.memset(vals[:, :, 2:3], 1.0).then_inc(small_ok, 1)
            dve.wait_ge(pairs_in, 16)
            link(v.tensor_copy(pair_f[:, :, :], pair_i[:, :].rearrange("p (c t) -> p t c", t=2)))
            link(v.tensor_scalar(tmp_e[:, :, :], pair_f[:, :, :], 0.0, float(N), ALU.is_lt, ALU.mult))
            link(v.tensor_tensor(pair_f[:, :, :], pair_f[:, :, :], tmp_e[:, :, :], ALU.add))
            link(v.tensor_scalar(tmp_e[:, :, :], pair_f[:, :, :], 0.0, None, ALU.is_ge))
            link(v.scalar_tensor_tensor(tmp_e[:, :, :], pair_f[:, :, :], float(N), tmp_e[:, :, :], ALU.is_lt, ALU.mult))
            link(v.tensor_tensor(valid[:, :], pair_f[:, 0, :], pair_f[:, 1, :], ALU.not_equal))
            link(v.tensor_tensor(valid[:, :], valid[:, :], tmp_e[:, 0, :], ALU.mult))
            link(v.tensor_tensor(valid[:, :], valid[:, :], tmp_e[:, 1, :], ALU.mult))
            link(v.tensor_tensor(pair_f[:, :, :], pair_f[:, :, :], valid[:, None, :].to_broadcast([EP, 2, EC]), ALU.mult))
            link(v.scalar_tensor_tensor(look_f[:, :], pair_f[:, 0, :], float(N), pair_f[:, 1, :], ALU.mult, ALU.add))
            v.tensor_copy(look_i[:, :], look_f[:, :]).then_inc(look_ok, 1)
            did.did(v.tensor_copy(vals[:, :, 0:2].rearrange("p c t -> p t c"), pair_f[:, :, :]))

            for k in range(KT):
                r = krows(k)
                dve.wait_ge(adj_in[k % STAGES], 16 * (k // STAGES + 1))
                v.tensor_copy(a16[0:r, k, :], adj32[k % STAGES][0:r, :]).then_inc(a16_ok, 1)
                dve.wait_ge(x_hi, k + 1)
                v.scalar_tensor_tensor(x16[0:r, 1, k, :], x32[0:r, k, :], XS, x16[0:r, 0, k, :],
                                       ALU.mult, ALU.subtract).then_inc(x_lo, 1)

            dve.wait_ge(deg_ps, 1)
            for rows, cols in ((P, slice(0, KT - 1)), (KREM, slice(KT - 1, KT))):
                src = psum[0:rows, DEG_BANK, cols]
                did.did(v.tensor_copy(deg[0:rows, cols], src))
                link(v.tensor_scalar(rzb[0:rows, cols], src, ALPHA, ALPHA1, ALU.mult, ALU.add))
                link(v.reciprocal(rzb[0:rows, cols], rzb[0:rows, cols]))
                did.did(v.tensor_scalar(cb[0:rows, cols], rzb[0:rows, cols], ALPHA, None, ALU.mult))
                v.tensor_scalar(gb[0:rows, cols], rzb[0:rows, cols], XS * ALPHA1, XS,
                                ALU.mult, ALU.add).then_inc(coef_ok, 1)

            def statistics(rows, src, k, ready, mark):
                dve.wait_ge(*mark)
                did.did(v.bn_stats(st[0:rows, k, :], src))
                did.wait(dve)
                v.bn_aggr(mv[0:rows, k, :], st[0:rows, k, :]).then_inc(ready, 1)

            def finish(i):
                r = krows(i)
                dve.wait_ge(sd_ok, i + 1)
                link(v.reciprocal(rs[0:r, i % 4:i % 4 + 1], sd[0:r, i % 4:i % 4 + 1]))
                v.tensor_scalar(x2[0:r, i, :], z[0:r, i % 3, :], mv[0:r, i % 4, 0:1], rs[0:r, i % 4:i % 4 + 1],
                                ALU.subtract, ALU.mult).then_inc(x2_ok, 1)

            def low(i):
                r = krows(i)
                dve.wait_ge(x2_hi, i + 1)
                v.scalar_tensor_tensor(x216[0:r, 1, i, :], x2[0:r, i, :], XS / YS, x216[0:r, 0, i, :],
                                       ALU.mult, ALU.subtract).then_inc(x2_lo, 1)

            dve.wait_ge(coef_ok, 2)
            for i in range(KT):
                r = krows(i)
                dve.wait_ge(l0_ps, i + 1)
                dve.wait_ge(tx_ok, i + 1)
                v.scalar_tensor_tensor(z[0:r, i % 3, :], psum[0:r, L0_BANK[i], :], cb[0:r, i:i + 1], tx[0:r, i % 2, :],
                                       ALU.mult, ALU.add).then_inc(z_ok, 1)
                statistics(r, z[0:r, i % 3, :], i % 4, var_ok, (z_ok, i + 1))
                if i >= 1:
                    finish(i - 1)
                if i >= 2:
                    low(i - 2)
            finish(KT - 1)
            low(KT - 2)
            low(KT - 1)
            dve.wait_ge(w_hi, 1)
            v.scalar_tensor_tensor(w16[:, 1, :, :].rearrange("p t n -> p (t n)"), w32.rearrange("p t n -> p (t n)"), WS,
                                   w16[:, 0, :, :].rearrange("p t n -> p (t n)"), ALU.mult, ALU.subtract).then_inc(w_lo, 1)
            dve.wait_ge(bt_in, 32)
            link(v.tensor_scalar(bt[:, :], bt[:, :], WS, None, ALU.mult))
            dve.wait_ge(checks, 1)

            def agg_low(n):
                t, c = BLOCKS[n]
                c0, w = CHUNKS[c]
                dve.wait_ge(agg_hi, n + 1)
                v.scalar_tensor_tensor(agg16[:, 1, t, c0:c0 + w], psum[:, A_BANK[n % 6], 0:w], AS / XS,
                                       agg16[:, 0, t, c0:c0 + w], ALU.mult, ALU.subtract).then_inc(agg_lo, 1)

            for n in range(7):
                agg_low(n)
            dve.wait_ge(looked_in, 16 * EC)
            dve.wait_ge(pool_chain, POOL_STEPS)
            link(v.scalar_tensor_tensor(active[:, :], looked[:, :], 1.0, valid[:, :], ALU.is_equal, ALU.mult))
            link(v.tensor_tensor_scan(upto[:, :], active[:, :], zero_e[:, :], 0.0, ALU.add, ALU.add))
            v.tensor_copy(total16[:, :], upto[:, EC - 1:EC]).then_inc(total_ok, 1)
            agg_low(7)
            dve.wait_ge(off_ps, 1)
            did.did(v.tensor_copy(seen[:, 4:5], psum[:, 2, 1:2]))
            link(v.scalar_tensor_tensor(pos[:, :], upto[:, :], psum[0:EP, 2, 0:1], active[:, :], ALU.add, ALU.mult))
            link(v.tensor_scalar(pos16[:, :], pos[:, :], 100.0, None, ALU.min))
            v.tensor_tensor(one_slot, pos16[:, :].unsqueeze(2).to_broadcast([EP, EC, HALF]),
                            cap[:, None, :].to_broadcast([EP, EC, HALF]), ALU.is_equal).then_inc(one_ok, 1)
            agg_low(8)
            dve.wait_ge(slot_ps, 1)
            link(v.tensor_copy(slot16[:, :], psum[0:HALF, 3, 0:3]))
            v.tensor_tensor(spread[:, :, :, :].rearrange("p t q s -> p t (q s)"),
                            slot16[:, :].unsqueeze(2).to_broadcast([HALF, 3, P]),
                            twice16[:, None, :, :].rearrange("p o q s -> p o (q s)").to_broadcast([HALF, 3, P]),
                            ALU.mult).then_inc(slot_ok, 1)
            agg_low(9)
            dve.wait_ge(across_ps, 1)
            link(v.tensor_copy(slot[:, :], psum[:, 2, 384:387]))
            v.tensor_copy(slot_i[:, :], slot[:, 0:2]).then_inc(index_ok, 1)
            link(v.tensor_copy(across[:, :, :], psum[:, 2, 0:384].rearrange("p (t s) -> p t s", s=P)))
            v.scalar_tensor_tensor(rowm[:, :], across[:, 0, :], slot[:, 0:1], across[:, 2, :],
                                   ALU.is_equal, ALU.mult).then_inc(rowm_ok, 1)
            dve.wait_ge(rowm_ok, 1)
            link(v.scalar_tensor_tensor(pairm[:, :], across[:, 1, 0:HALF], slot[:, 1:2], rowm[:, 0:HALF],
                                        ALU.is_equal, ALU.mult))
            did.did(v.tensor_scalar(rowoff[:, :], rowm[:, 0:HALF], -1.0, BIG, ALU.add, ALU.mult))
            link(v.tensor_tensor(pairm[:, :], pairm[:, :], lower[:, :], ALU.mult))
            did.did(v.tensor_reduce(later[:, 0:1], pairm[:, :], AX.X, ALU.max))
            link(v.tensor_tensor(junk[:, :], rowm[:, 0:HALF], lower[:, :], ALU.mult))
            link(v.tensor_reduce(later[:, 1:2], junk[:, :], AX.X, ALU.max))
            link(v.tensor_scalar(ul[:, :], later[:, :], -1.0, 1.0, ALU.mult, ALU.add))
            link(v.tensor_scalar(ul[:, :], ul[:, :], slot[:, 2:3], None, ALU.mult))
            link(v.tensor_scalar(used32[:, :], slot[:, 2:3], AS, None, ALU.mult))
            v.tensor_scalar(oh16[:, :], iota16[:, :], slot[:, 0:1], YS / XS, ALU.is_equal, ALU.mult).then_inc(oh_ok, 1)
            agg_low(10)
            agg_low(11)
            dve.wait_ge(acol_in, 16)
            v.tensor_scalar(ac16[:, :], a_col, used32[:, 0:1], last32[:, 0:1], ALU.mult, ALU.add).then_inc(ac_ok, 1)
            dve.wait_ge(kb_ok, 1)
            for t in range(DT):
                last = v.scalar_tensor_tensor(qk[:, t, :], psum[:, 2, t * HALF:(t + 1) * HALF], bqk[:, 0, t:t + 1],
                                              kb[:, t, :], ALU.add, ALU.mult)
            last.then_inc(qk_ok, 1)
            dve.wait_ge(sT_ps, 1)
            scores = psum[:, 3, :].rearrange("p (h s) -> p h s", s=HALF)
            did.did(v.tensor_tensor(sI[:, :, :], scores, same[:, None, :].to_broadcast([P, HEADS, HALF]), ALU.mult))
            v.tensor_tensor(sT[:, :, :], scores, rowm[:, None, 0:HALF].to_broadcast([P, HEADS, HALF]),
                            ALU.mult).then_inc(sT_used, 1)
            dve.wait_ge(sT_used, 1)
            link(v.tensor_tensor(sT[:, :, :], sT[:, :, :], rowoff[:, None, :].to_broadcast([P, HEADS, HALF]), ALU.add))
            did.did(v.tensor_reduce(mx[:, :], sT[:, :, :], AX.X, ALU.max))
            link(v.tensor_reduce(arg[:, 0, :], sI[:, :, :], AX.X, ALU.add))
            link(v.tensor_scalar(mx[:, :], mx[:, :], DIAG, None, ALU.max))
            did.did(v.tensor_scalar(arg[:, 1, :], mx[:, :], -1.0, None, ALU.mult))
            did.did(v.tensor_scalar(arg[:, 2, :], mx[:, :], -1.0, DIAG, ALU.mult, ALU.add))
            link(v.tensor_tensor(arg[:, 0, :], arg[:, 0, :], mx[:, :], ALU.subtract))
            v.tensor_scalar(arg[:, 0, :], arg[:, 0, :], 0.0, None, ALU.min).then_inc(arg_ok, 1)
            dve.wait_ge(ex_ok, 1)
            link(v.tensor_copy(exu[:, HEADS:HEADS + 1], ul[:, 0:1]))
            v.tensor_scalar(exu[:, 0:HEADS], ex[:, 0, :], ul[:, 0:1], None, ALU.mult).then_inc(exu_ok, 1)
            dve.wait_ge(zz_ps, 1)
            dve.wait_ge(ar_ok, 1)
            link(v.tensor_scalar(nn[:, :], nrow[:, :], 1.0, psum[:, 1, HEADS:HEADS + 1], ALU.subtract, ALU.subtract))
            link(v.scalar_tensor_tensor(zz[:, :], ex[:, 1, :], nn[:, 0:1], ex[:, 2, :], ALU.mult, ALU.add))
            link(v.tensor_tensor(zz[:, :], zz[:, :], psum[:, 1, 0:HEADS], ALU.add))
            link(v.reciprocal(zz[:, :], zz[:, :]))
            did.did(v.tensor_tensor(arg[:, 0:2, :], ex[:, 1:3, :], zz[:, None, :].to_broadcast([P, 2, HEADS]), ALU.mult))
            link(v.tensor_tensor(arg[:, 2, :], exu[:, 0:HEADS], zz[:, :], ALU.mult))
            link(v.tensor_reduce(cdw[:, :], arg[:, :, :], AX.X, ALU.add))
            link(v.tensor_scalar(cdw[:, :], cdw[:, :], 1.0 / HEADS, None, ALU.mult))
            link(v.scalar_tensor_tensor(sm[:, 0:1], cdw[:, 0:1], ul[:, 0:1], cdw[:, 2:3], ALU.mult, ALU.subtract))
            v.tensor_scalar(xoc[:, :], xo[0:HALF, :], sm[0:HALF, 0:1], -1.0, ALU.mult, ALU.mult).then_inc(xoc_ok, 1)
            link(v.tensor_tensor(sm[:, 1:2], cdw[:, 1:2], cdw[:, 0:1], ALU.subtract))
            did.did(v.tensor_scalar(sm[:, 3:4], sm[:, 1:2], XS, XS, ALU.mult, ALU.add))
            link(v.tensor_scalar(sm[:, 4:5], nrow[:, :], ALPHA, ALPHA1, ALU.mult, ALU.add))
            link(v.reciprocal(sm[:, 4:5], sm[:, 4:5]))
            did.did(v.tensor_scalar(sm[:, 5:6], sm[:, 4:5], ALPHA, None, ALU.mult))
            v.tensor_scalar(sm[:, 7:8], sm[:, 4:5], XS * ALPHA1, XS, ALU.mult, ALU.add).then_inc(coefe_ok, 1)
            dve.wait_ge(txe_ok, 2)
            dve.wait_ge(axe_ps, 1)
            link(v.scalar_tensor_tensor(ze[:, 1, :], psum[:, 3, :], sm[:, 5:6], txe[:, 1, :], ALU.mult, ALU.add))
            did.did(v.bn_stats(ste[:, 1, :], ze[:, 1, :]))
            link(v.scalar_tensor_tensor(ze[:, 0, :], psum[:, 3, :], cdw[:, 0:1], txe[:, 0, :], ALU.mult, ALU.add))
            dve.wait_ge(corr_ps, 1)
            link(v.scalar_tensor_tensor(ze[:, 0, :], psum[:, 2, :], XS, ze[:, 0, :], ALU.mult, ALU.add))
            did.did(v.bn_aggr(mve[:, 1, :], ste[:, 1, :]))
            link(v.bn_stats(ste[:, 0, :], ze[:, 0, :]))
            v.bn_aggr(mve[:, 0, :], ste[:, 0, :]).then_inc(ze_ok, 1)
            dve.wait_ge(sde_ok, 1)
            link(v.reciprocal(rse[:, :], sde[:, :]))
            link(v.tensor_scalar(rse[:, :], rse[:, :], ul[:, 1:2], None, ALU.mult))
            for a in range(2):
                did.did(v.tensor_scalar(ze[:, a, :], ze[:, a, :], mve[:, a, 0:1], rse[:, a:a + 1],
                                        ALU.subtract, ALU.mult))
            did.wait(dve)
            v.tensor_tensor(delta[:, :], ze[:, 0, :], ze[:, 1, :], ALU.subtract).then_inc(delta_ok, 1)
            dve.wait_ge(delta_ok, 1)
            did.did(v.tensor_copy(d16[0:HALF, :], delta[0:HALF, :]))
            link(v.tensor_copy(hi_tmp[HALF:P, 0, :], delta[HALF:P, :]))
            v.tensor_tensor(d16[HALF:P, :], delta[HALF:P, :], hi_tmp[HALF:P, 0, :], ALU.subtract).then_inc(d16_ok, 1)
            dve.wait_ge(dT_hi, 1)
            v.tensor_tensor(dT16[:, 1, :, :].rearrange("p t n -> p (t n)"), psum[:, 3, :],
                            dT16[:, 0, :, :].rearrange("p t n -> p (t n)"), ALU.subtract).then_inc(dT_lo, 1)
            dve.wait_ge(dw_ps, 1)
            v.scalar_tensor_tensor(vv[:, :], psum[:, 1, :], 1.0 / XS, bt[:, :], ALU.mult, ALU.add).then_inc(v_ok, 1)
            dve.wait_ge(v_ok, 1)
            did.did(v.tensor_copy(v16[0:HALF, :], vv[0:HALF, :]))
            link(v.tensor_copy(hi_tmp[HALF:P, 1, :], vv[HALF:P, :]))
            v.tensor_tensor(v16[HALF:P, :], vv[HALF:P, :], hi_tmp[HALF:P, 1, :], ALU.subtract).then_inc(v16_ok, 1)

            def limits():
                dve.wait_ge(vsq_ok, 1)
                did.did(v.tensor_reduce(seen[:, 0:1], adj_off[:, :], AX.X, ALU.add))
                did.did(v.tensor_reduce(seen[:, 1:2], x_sq[:, :], AX.X, ALU.max))
                link(v.tensor_reduce(seen[:, 3:4], deg[:, :], AX.X, ALU.max))
                link(v.tensor_tensor(kept[:, :], seen[:, :], limit[:, :], ALU.is_le))
                link(v.tensor_reduce(kept1[:, :], kept[:, :], AX.X, ALU.min))
                v.tensor_copy(kept16[:, :], kept1[:, :]).then_inc(kept_ok, 1)

            def flag_out():
                dve.wait_ge(kept_ps, 1)
                v.tensor_scalar(flag[0:1, 0:1], psum[0:1, 1, 0:1], P - 0.5, None, ALU.is_lt).then_inc(flag_ok, 1)
                dve.wait_ge(flag_ok, 1)

            def finish2(i):
                r = krows(i)
                dve.wait_ge(sd2_ok, i + 1)
                link(v.reciprocal(rs[0:r, i % 4:i % 4 + 1], sd[0:r, i % 4:i % 4 + 1]))
                if i >= 3:
                    dve.wait_ge(out_done[i % 3], 16 * (i // 3))
                v.tensor_scalar(y[0:r, i % 3, :], z[0:r, i % 3, :], mv[0:r, i % 4, 0:1], rs[0:r, i % 4:i % 4 + 1],
                                ALU.subtract, ALU.mult).then_inc(y_ok, 1)

            for i in range(KT):
                r = krows(i)
                dve.wait_ge(y_ps, i + 1)
                v.scalar_tensor_tensor(z[0:r, i % 3, :], psum[0:r, Y_BANK[i], :], 0.0, x2[0:r, i, :],
                                       ALU.max, ALU.add).then_inc(y_used, 1)
                dve.wait_ge(y_used, i + 1)
                dve.wait_ge(r_ps, i + 1)
                v.tensor_tensor(z[0:r, i % 3, :], psum[0:r, R_BANK[i], :], z[0:r, i % 3, :], ALU.add).then_inc(z2_ok, 1)
                statistics(r, z[0:r, i % 3, :], i % 4, var2_ok, (z2_ok, i + 1))
                if i >= 1:
                    finish2(i - 1)
                if i == 1:
                    limits()
                if i == 3:
                    flag_out()
            finish2(KT - 1)

        @block.tensor
        def _(pe):
            mm = nc.tensor.matmul

            def layer_one(i, k):
                m, r = krows(i), krows(k)
                for h in range(2):
                    last = mm(psum[0:m, L0_BANK[i], :], a16[0:r, k, i * P:i * P + m], x16[0:r, h, k, :],
                              start=(k == 0 and h == 0), stop=(k == KT - 1 and h == 1))
                return last

            pe.wait_ge(pool_chain, 1)
            for k in range(KT):
                r = krows(k)
                pe.wait_ge(a16_ok, k + 1)
                for i in range(KT):
                    m = krows(i)
                    last = mm(psum[0:m, DEG_BANK, i:i + 1], a16[0:r, k, i * P:i * P + m], ones16[0:r, 0:1],
                              start=(k == 0 and i == 0), stop=(k == KT - 1 and i == KT - 1), skip_group_check=True)
                if k == KT - 1:
                    last.then_inc(deg_ps, 1)
                pe.wait_ge(x_lo, k + 1)
                for i in range(G1):
                    last = layer_one(i, k)
                    if k == KT - 1:
                        last.then_inc(l0_ps, 1)
            for i in range(G1, KT):
                if i > G1:
                    pe.wait_ge(z_ok, i - G1)
                for k in range(KT):
                    last = layer_one(i, k)
                last.then_inc(l0_ps, 1)

            def layer_two(n, k):
                t, c = BLOCKS[n]
                c0, w = CHUNKS[c]
                r = krows(k)
                for h in range(2):
                    last = mm(psum[:, A_BANK[n % 6], 0:w], x216[0:r, h, k, t * P:(t + 1) * P], a16[0:r, k, c0:c0 + w],
                              start=(k == 0 and h == 0), stop=(k == KT - 1 and h == 1))
                return last

            pe.wait_ge(coef_ok, 2)
            for k in range(KT - 1):
                pe.wait_ge(x2_lo, k + 1)
                for n in range(G1):
                    if k == 0:
                        pe.wait_ge(z_ok, {4: 5, 5: 6, 6: 6, 7: 7, 0: 8, 1: 9}[A_BANK[n]])
                    layer_two(n, k)
            pe.wait_ge(x2_lo, KT)
            for n in range(G1):
                layer_two(n, KT - 1).then_inc(agg_ps, 1)

            def block_two(n):
                pe.wait_ge(agg_lo, n - G1 + 1)
                for k in range(KT):
                    last = layer_two(n, k)
                last.then_inc(agg_ps, 1)

            block_two(6)
            block_two(7)
            pe.wait_ge(total_ok, 1)
            mm(psum[0:EP, 2, 0:1], tri[:, :], total16[:, :], start=True, stop=True)
            mm(psum[:, 2, 1:2], ones16[0:EP, :], total16[:, :], start=True, stop=True).then_inc(off_ps, 1)
            block_two(8)
            pe.wait_ge(one_ok, 1)
            for c in range(EC):
                last = mm(psum[0:HALF, 3, 0:3], one_slot[:, c, :], vals[:, c, :], start=(c == 0), stop=(c == EC - 1))
            last.then_inc(slot_ps, 1)
            block_two(9)
            pe.wait_ge(slot_ok, 1)
            mm(psum[:, 2, 0:384], ones16[0:HALF, :], spread[:, :, :, :].rearrange("p t q s -> p (t q s)"),
               start=True, stop=True)
            mm(psum[:, 2, 384:387], twice16[:, :, :].rearrange("p q s -> p (q s)"), slot16[:, :],
               start=True, stop=True).then_inc(across_ps, 1)
            block_two(10)
            block_two(11)
            pe.wait_ge(xs_in, 16)
            pe.wait_ge(xo_in, 16)
            for n, t_rows in enumerate((xs, xo)):
                for t in range(DT):
                    last = nc.tensor.transpose(psum[:, 3, (n * DT + t) * HALF:(n * DT + t + 1) * HALF],
                                               t_rows[0:HALF, t * P:(t + 1) * P], ident[0:HALF, 0:HALF])
            last.then_inc(xsoT_ps, 1)

            def out_tile(i):
                m = krows(i)
                for t in range(DT):
                    for h, hw in ((0, 0), (0, 1), (1, 0)):
                        mm(psum[0:m, Y_BANK[i], :], agg16[:, h, t, i * P:i * P + m], w16[:, hw, t, :],
                           start=(t == 0 and (h, hw) == (0, 0)), stop=False)

            pe.wait_ge(agg_lo, 12)
            pe.wait_ge(w_lo, 1)
            out_tile(0)
            pe.wait_ge(xsoT_ok, 1)
            pe.wait_ge(wqk_in, 32)
            for w in range(2):
                for to in range(DT):
                    for t in range(DT):
                        last = mm(psum[:, 2, (w * DT + to) * HALF:(w * DT + to + 1) * HALF],
                                  wqk[:, w, t, to * P:(to + 1) * P], xsoT[:, w * DT + t, :],
                                  start=(t == 0), stop=(t == DT - 1))
            last.then_inc(qk_ps, 1)
            out_tile(1)
            pe.wait_ge(qk_ok, 1)
            for h in range(HEADS):
                last = mm(psum[:, 3, h * HALF:(h + 1) * HALF], hsel[:, h % 2, :], qk[:, h // 2, :],
                          start=True, stop=True)
            last.then_inc(sT_ps, 1)
            out_tile(2)
            pe.wait_ge(ar_ok, 1)
            for k in range(KT):
                r = krows(k)
                bank = psum[:, 2 if k < 8 else 1, :].bitcast(F16)
                last = nc.tensor.transpose(bank[0:r, (k % 8) * P:(k % 8 + 1) * P], ar16[:, k * P:k * P + r], ident16[:, :])
            last.then_inc(arT_ps, 1)
            out_tile(3)
            pe.wait_ge(arT_ok, 3)
            pe.wait_ge(exu_ok, 1)
            pe.wait_ge(sT_used, 1)
            mm(psum[:, 1, 0:HEADS + 1], rowm[0:HALF, :], exu[0:HALF, :], start=True, stop=True).then_inc(zz_ps, 1)
            for k in range(KT):
                r = krows(k)
                for h in range(2):
                    last = mm(psum[:, 3, :], arT[0:r, k, :], x16[0:r, h, k, :],
                              start=(k == 0 and h == 0), stop=(k == KT - 1 and h == 1))
            last.then_inc(axe_ps, 1)
            out_tile(4)
            pe.wait_ge(xoc_ok, 1)
            mm(psum[:, 2, :], rowm[0:HALF, :], xoc[:, :], start=True, stop=True).then_inc(corr_ps, 1)
            pe.wait_ge(delta_ok, 1)
            for t in range(DT):
                last = nc.tensor.transpose(psum[:, 3, t * P:(t + 1) * P], delta[:, t * P:(t + 1) * P], ident[:, :])
            last.then_inc(dT_ps, 1)
            pe.wait_ge(dT_lo, 1)
            pe.wait_ge(coefe_ok, 1)
            for t in range(DT):
                for h, hw in ((0, 0), (0, 1), (1, 0)):
                    last = mm(psum[:, 1, :], dT16[:, h, t, :], w16[:, hw, t, :],
                              start=(t == 0 and (h, hw) == (0, 0)), stop=(t == DT - 1 and h == 1))
            last.then_inc(dw_ps, 1)
            pe.wait_ge(v16_ok, 1)
            pe.wait_ge(ac_ok, 1)
            pe.wait_ge(oh_ok, 1)
            pe.wait_ge(d16_ok, 1)
            for i in range(KT):
                m = krows(i)
                mm(psum[0:m, Y_BANK[i], :], ac16[:, i * P:i * P + m], v16[:, :], start=False, stop=True).then_inc(y_ps, 1)
                if i >= 2:
                    pe.wait_ge(z2_ok, i - 1)
                mm(psum[0:m, R_BANK[i], :], oh16[:, i * P:i * P + m], d16[:, :], start=True, stop=True).then_inc(r_ps, 1)
                if i + YB < KT:
                    pe.wait_ge(y_used, i + 1)
                    out_tile(i + YB)
                if i == 2:
                    pe.wait_ge(kept_ok, 1)
                    mm(psum[0:P, 1, 0:1], ones16[:, :], kept16[:, :], start=True, stop=True).then_inc(kept_ps, 1)


def build(nc, x, adj, pairs, bq, bk, b, diag, xT, adjT, wqT, wkT, wT, x2d, out):
    with ExitStack() as ctx:
        flag = ctx.enter_context(nc.sbuf_tensor("flag", [1, 1], I32))
        fast_path(nc, flag, x, adj, adjT, diag, pairs, wqT, bq, wkT, bk, wT, b, out)
        general_path(nc, flag, None, x, xT, adj, adjT, pairs, wqT, bq, wkT, bk, wT, b, x2d, out)


def kernel(**inputs):
    import numpy as _np
    import concourse.bacc as _bacc
    from concourse import mybir as _mybir
    from concourse.bass_utils import run_bass_kernel_spmd as _run

    nc = _bacc.Bacc("TRN2", target_bir_lowering=False, num_devices=1)
    given = {
        "x": inputs["x"], "adj": inputs["adj"], "pairs": inputs["L0_gnn_rel_pair_index"],
        "bq": inputs["L0_gnn_bq"], "bk": inputs["L0_gnn_bk"], "b": inputs["L1_gnn_b"],
        "diag": _np.diagonal(inputs["adj"]), "xT": _np.asarray(inputs["x"]).T, "adjT": _np.asarray(inputs["adj"]).T,
        "wqT": _np.asarray(inputs["L0_gnn_Wq"]).T, "wkT": _np.asarray(inputs["L0_gnn_Wk"]).T,
        "wT": _np.asarray(inputs["L1_gnn_W"]).T,
    }
    arrays, aps = {}, {}
    for name, a in given.items():
        a = _np.ascontiguousarray(a)
        arrays["in_" + name] = a
        aps[name] = nc.dram_tensor("in_" + name, a.shape, _mybir.dt.from_np(a.dtype), kind="ExternalInput").ap()
    out = nc.dram_tensor("out", (N, D), F32, kind="ExternalOutput").ap()
    x2d = nc.dram_tensor("x2d", (N, D), F32, kind="Internal").ap()
    build(nc, x2d=x2d, out=out, **aps)
    r = _run(nc, [arrays], core_ids=[0])
    return r.results[0]["out"]
```

```python
import numpy as np
import concourse.bass as bass
from concourse import mybir
from contextlib import ExitStack

F32 = mybir.dt.float32
F16 = mybir.dt.float16
I32 = mybir.dt.int32
ALU = mybir.AluOpType
ACT = mybir.ActivationFunctionType
AX = mybir.AxisListType

N = 1354
D = 512
E = 10000
HEADS = 8
DK = D // HEADS
P = 128
DT = D // P
KT = -(-N // P)
KREM = N - (KT - 1) * P
EP, EC = 125, 80
assert EP * EC == E
EPS = 1e-5
DIAG = 1e-7
BIG = 3e38

GT = 11
GS = (N - P) // (GT - 1) + 1
GP = N - (GT - 1) * GS
assert GP <= P and GP >= GS
CHUNKS = [(c, min(512, N - c)) for c in range(0, N, 512)]


STAGES = 4
HALF = 64
SLOTS = HALF - 1
XS = 1024.0
AS = 32.0
WS = 256.0
YS = AS * WS
ALPHA = float(np.exp(np.float32(-DIAG)))
ALPHA1 = float(-np.expm1(-DIAG))
X_SQ_MAX = 3600.0
W_SQ_MAX = 5e4
DEG_MAX = 90.0
V_SQ_MAX = 3e9
BATCHES = [(0, 60), (60, 77), (77, EC)]
WARM = 9
CATCH_UP = 6
CLOSE_UP = (3, 5)
PREFIX_AT = 7
AT = [4, 10, 14, 17, 28, 30, 34, 47, 56]
ZB = 4
ZDEG, ZMEAN, ZVAR, ZROOT = range(D, D + 4)
ZW = D + 4
C32 = 4 * P + 1
C16 = N + P + EP + HALF + P
G1 = 6
FIRST = [(0, 3 * P), (3 * P, G1 * P)]


def krows(k):
    return P if k < KT - 1 else KREM


class Steps:

    def __init__(self, sem):
        self.sem, self.base, self.n = sem, 0, 0

    def did(self, ins):
        self.n += 1
        ins.then_inc(self.sem, 1)

    def wait(self, eng):
        eng.wait_ge(self.sem, self.base + self.n)


def general_path(nc, flag, flag_ready, x, xT, adj, adjT, pairs, wqT, bq, wkT, bk, wT, b, x2d, out):
    ctx = ExitStack()
    with ctx:
        def sb(name, shape, dt=F32):
            return ctx.enter_context(nc.sbuf_tensor("g_" + name, shape, dt))

        def sem(name):
            return ctx.enter_context(nc.semaphore("g_" + name))

        xT_sb = sb("xT", [P, DT, N])
        x_sb = sb("x", [P, KT, D])
        w1_sb = sb("w1", [P, DT, D])
        w2_sb = sb("w2", [P, DT, D])
        kh = sb("kh", [DK, HEADS, N])
        qh = sb("qh", [DK, HEADS, GP])
        bqk = sb("bqk", [DK, 2, HEADS])
        brow = sb("brow", [1, D])
        ones_row = sb("ones_row", [1, P])
        pair_i = sb("pair_i", [EP, 2 * EC], I32)
        pair_f = sb("pair_f", [EP, 2, EC])
        neg = sb("neg", [EP, 2, EC])
        one_sub = sb("one_sub", [EP, EC, GP], F16)
        one_obj = sb("one_obj", [EP, 2, N], F16)
        zero16 = sb("zero16", [EP, GP], F16)
        zeroN = sb("zeroN", [EP, 512], F16)
        iota16 = sb("iota16", [P, N], F16)
        col_row = sb("col_row", [GP, N])
        ident = sb("ident", [P, P])
        a_t = sb("a_t", [GP, N])
        on_diag = sb("on_diag", [GP, N])
        edge = sb("edge", [GP, N])
        s_t = sb("s_t", [GP, N])
        p_t = sb("p_t", [GP, N])
        f_t = sb("f_t", [GP, N])
        fT = sb("fT", [P, KT, GP])
        xt = sb("xt", [GP, D])
        z_t = sb("z_t", [GP, D])
        y_t = sb("y_t", [GP, D])
        st = sb("st", [GP, 6])
        mv = sb("mv", [GP, 2])
        sm = sb("sm", [GP, 8])
        token = sb("token", [1, 16])
        agg = a_t[:, 0:D]
        aggT = on_diag
        aT = xT_sb
        psum = ctx.enter_context(nc.psum_tensor("g_psum", [P, 8, 512], F32))
        pflat = psum[:, :, :].rearrange("p b n -> p (b n)")
        even, odd = pflat[:, 0:N], pflat[:, 1536:1536 + N]

        loaded = sem("loaded")
        consts = sem("consts")
        pool_chain = sem("pool_chain")
        kproj = sem("kproj")
        kproj_used = sem("kproj_used")
        tile_in = sem("tile_in")
        q_bias = sem("q_bias")
        q_ps = sem("q_ps")
        q_sb = sem("q_sb")
        sub_ready = sem("sub_ready")
        obj_ready = sem("obj_ready")
        obj_free = sem("obj_free")
        em_ps = sem("em_ps")
        em_used = sem("em_used")
        s_ps = sem("s_ps")
        s_used = sem("s_used")
        s_ok = sem("s_ok")
        p_ok = sem("p_ok")
        f_ok = sem("f_ok")
        fT_ps = sem("fT_ps")
        fT_sb = sem("fT_sb")
        o_ps = sem("o_ps")
        z_ok = sem("z_ok")
        var_ok = sem("var_ok")
        std_ok = sem("std_ok")
        y_ok = sem("y_ok")
        y_out = sem("y_out")
        chain = sem("chain")
        x2_in = sem("x2_in")
        t2_in = sem("t2_in")
        agg_ps = sem("agg_ps")
        agg_sb = sem("agg_sb")
        aggT_ps = sem("aggT_ps")
        aggT_sb = sem("aggT_sb")
        out_ps = sem("out_ps")
        relu_ok = sem("relu_ok")
        z2_ok = sem("z2_ok")
        var2_ok = sem("var2_ok")
        std2_ok = sem("std2_ok")
        y2_ok = sem("y2_ok")
        y2_out = sem("y2_out")
        chain2 = sem("chain2")

        LOADS = 10
        block = ctx.enter_context(nc.Block())

        def flagged(eng):
            if flag is None:
                return None
            if flag_ready is not None:
                eng.wait_ge(flag_ready, 1)
            return eng.value_load(flag[0:1, 0:1], min_val=0, max_val=1)

        @block.sync
        def _(sp):
            def body():
                def load(dst, src):
                    sp.dma_start(dst, src).then_inc(loaded, 16)

                load(xT_sb[:, :, :], xT.rearrange("(t p) n -> p t n", p=P))
                load(w1_sb[:, :, :], wkT.rearrange("(t p) n -> p t n", p=P))
                load(w2_sb[:, :, :], wqT.rearrange("(t p) n -> p t n", p=P))
                load(x_sb[:, 0:KT - 1, :], x[0:(KT - 1) * P, :].rearrange("(t p) n -> p t n", p=P))
                load(x_sb[0:KREM, KT - 1, :], x[(KT - 1) * P:N, :])
                load(pair_i[:, :], pairs.rearrange("(p c) t -> p (c t)", p=EP))
                load(brow[0:1, :], b.rearrange("(o n) -> o n", o=1))
                with nc.allow_non_contiguous_dma(reason="two small bias vectors"):
                    load(bqk[:, 0, :], bq.rearrange("(h d) -> d h", d=DK))
                    load(bqk[:, 1, :], bk.rearrange("(h d) -> d h", d=DK))
                load(xt[0:1, :], x[0:1, :])
                sp.wait_ge(loaded, 16 * LOADS)
                with sp.Fori(0, GT) as i:
                    row = sp.snap(i * GS)
                    sp.wait_ge(y_ok, i + 1)
                    sp.dma_start(a_t[:, :], adj[bass.ds(row, GP), :]).then_inc(tile_in, 16)
                    sp.dma_start(xt[:, :], x[bass.ds(row, GP), :]).then_inc(tile_in, 16)
                    sp.wait_ge(y_ok, i + 2)
                    sp.dma_start(x2d[bass.ds(row, GP), :], y_t[:, :]).then_inc(y_out, 16)
                sp.wait_ge(y_out, 16 * GT + 16)
                sp.dma_start(x_sb[:, 0:KT - 1, :],
                             x2d[0:(KT - 1) * P, :].rearrange("(t p) n -> p t n", p=P)).then_inc(x2_in, 16)
                sp.dma_start(x_sb[0:KREM, KT - 1, :], x2d[(KT - 1) * P:N, :]).then_inc(x2_in, 16)
                sp.dma_start(w1_sb[:, :, :], wT.rearrange("(t p) n -> p t n", p=P)).then_inc(x2_in, 16)
                with sp.Fori(0, GT) as i:
                    row = sp.snap(i * GS)
                    sp.wait_ge(y2_ok, i + 1)
                    aTv = aT.rearrange("p t n -> p (t n)")
                    aTv = aTv[:, 0:KT * GP].rearrange("p (t n) -> p t n", n=GP)
                    sp.dma_start(aTv[:, 0:KT - 1, :],
                                 adjT[0:(KT - 1) * P, bass.ds(row, GP)]
                                 .rearrange("(t p) n -> p t n", p=P)).then_inc(t2_in, 16)
                    sp.dma_start(aTv[0:KREM, KT - 1, :],
                                 adjT[(KT - 1) * P:N, bass.ds(row, GP)]).then_inc(t2_in, 16)
                    sp.dma_start(xt[:, :], x2d[bass.ds(row, GP), :]).then_inc(t2_in, 16)
                    sp.wait_ge(y2_ok, i + 2)
                    sp.dma_start(out[bass.ds(row, GP), :], y_t[:, :]).then_inc(y2_out, 16)
                sp.wait_ge(y2_out, 16 * GT + 16)

            v = flagged(sp)
            if v is None:
                body()
            else:
                with sp.If(v != 0):
                    body()

        @block.gpsimd
        def _(pool):
            def body():
                nc.gpsimd.iota(iota16[:, :], [[1, N]], base=0, channel_multiplier=0,
                               allow_small_or_imprecise_dtypes=True).then_inc(consts, 1)
                nc.gpsimd.iota(col_row[:, :], [[1, N]], base=0, channel_multiplier=-1,
                               allow_small_or_imprecise_dtypes=True).then_inc(consts, 1)
                nc.gpsimd.memset(ident[:, :], 0.0).then_inc(pool_chain, 1)
                nc.gpsimd.memset(zero16[:, :], 0.0).then_inc(consts, 1)
                nc.gpsimd.memset(zeroN[:, :], 0.0).then_inc(consts, 1)
                nc.gpsimd.memset(ones_row[:, :], 1.0).then_inc(consts, 1)
                pool.wait_ge(pool_chain, 1)
                nc.gpsimd.affine_select(out=ident[:, :], in_=ident[:, :], compare_op=ALU.not_equal, fill=1.0,
                                        base=0, pattern=[[-1, P]], channel_multiplier=1).then_inc(consts, 1)

            v = flagged(pool)
            if v is None:
                body()
            else:
                with pool.If(v != 0):
                    body()

        @block.tensor
        def _(pe):
            def body():
                pe.wait_ge(loaded, 16 * LOADS)
                pe.wait_ge(consts, 6)
                n = 0
                for h in range(HEADS):
                    for c, w in CHUNKS:
                        if n >= 2:
                            pe.wait_ge(kproj_used, n - 1)
                        for k in range(DT):
                            last = nc.tensor.matmul(psum[0:DK, n % 2, 0:w], w1_sb[:, k, h * DK:(h + 1) * DK],
                                                    xT_sb[:, k, c:c + w], start=(k == 0), stop=(k == DT - 1))
                        last.then_inc(kproj, 1)
                        n += 1
                pe.wait_ge(kproj_used, n)
                with pe.Fori(0, GT) as i:
                    for h in range(HEADS):
                        for k in range(DT):
                            last = nc.tensor.matmul(psum[0:DK, 6 + h // 4, (h % 4) * GP:(h % 4 + 1) * GP],
                                                    w2_sb[:, k, h * DK:(h + 1) * DK],
                                                    xT_sb[:, k, bass.ds(i * GS, GP)],
                                                    start=(k == 0), stop=(k == DT - 1))
                    last.then_inc(q_ps, 1)
                    pe.wait_ge(z_ok, i + 1)
                    pe.wait_ge(sub_ready, i + 1)
                    for c, w in CHUNKS:
                        nc.tensor.matmul(even[0:GP, c:c + w], zero16[:, :], zeroN[:, 0:w], start=True, stop=False)
                    with pe.Fori(0, EC // 2) as c2:
                        for u in range(2):
                            pe.wait_ge(obj_ready, i * EC + c2 * 2 + (u + 1))
                            for c, w in CHUNKS:
                                last = nc.tensor.matmul(even[0:GP, c:c + w], one_sub[:, bass.ds(c2 * 2 + u, 1), :].rearrange("p o n -> p (o n)"),
                                                        one_obj[:, u, c:c + w], start=False, stop=False)
                            last.then_inc(obj_free, 1)
                    for c, w in CHUNKS:
                        last = nc.tensor.matmul(even[0:GP, c:c + w], zero16[:, :], zeroN[:, 0:w], start=False, stop=True)
                    last.then_inc(em_ps, 1)
                    pe.wait_ge(q_sb, i + 1)
                    for h in range(HEADS):
                        if h == 0:
                            pe.wait_ge(em_used, i + 1)
                        elif h == 1:
                            pe.wait_ge(fT_sb, 4 * i + 4)
                        else:
                            pe.wait_ge(s_used, i * HEADS + (HEADS + h - 1))
                        s_bank = even if h % 2 == 0 else odd
                        for c, w in CHUNKS:
                            last = nc.tensor.matmul(s_bank[0:GP, c:c + w], qh[:, h, :], kh[:, h, c:c + w],
                                                    start=True, stop=True)
                        last.then_inc(s_ps, 1)
                    pe.wait_ge(f_ok, i + 1)
                    for k in range(KT):
                        r = krows(k)
                        last = nc.tensor.transpose(psum[0:r, 3 + k // 4, (k % 4) * P:(k % 4) * P + GP],
                                                   f_t[:, k * P:k * P + r], ident[0:GP, 0:GP])
                    last.then_inc(fT_ps, 1)
                    pe.wait_ge(fT_sb, 4 * i + 8)
                    for k in range(KT):
                        r = krows(k)
                        last = nc.tensor.matmul(psum[0:GP, 0, :], fT[0:r, k, :], x_sb[0:r, k, :],
                                                start=(k == 0), stop=(k == KT - 1))
                    last.then_inc(o_ps, 1)
                pe.wait_ge(z_ok, GT + 1)
                pe.wait_ge(x2_in, 48)
                with pe.Fori(0, GT) as i:
                    aTv = aT.rearrange("p t n -> p (t n)")
                    aTv = aTv[:, 0:KT * GP].rearrange("p (t n) -> p t n", n=GP)
                    pe.wait_ge(t2_in, 48 * i + 48)
                    for k in range(KT):
                        r = krows(k)
                        last = nc.tensor.matmul(psum[0:GP, 0, :], aTv[0:r, k, :], x_sb[0:r, k, :],
                                                start=(k == 0), stop=(k == KT - 1))
                    last.then_inc(agg_ps, 1)
                    pe.wait_ge(agg_sb, i + 1)
                    for k in range(DT):
                        last = nc.tensor.transpose(psum[:, 1, k * P:k * P + GP], agg[:, k * P:(k + 1) * P],
                                                   ident[0:GP, 0:GP])
                    last.then_inc(aggT_ps, 1)
                    pe.wait_ge(aggT_sb, i + 1)
                    nc.tensor.matmul(psum[0:GP, 2, :], ones_row[0:1, 0:GP], brow[0:1, :], start=True, stop=False)
                    for k in range(DT):
                        last = nc.tensor.matmul(psum[0:GP, 2, :], fT[:, k, :], w1_sb[:, k, :],
                                                start=False, stop=(k == DT - 1))
                    last.then_inc(out_ps, 1)

            v = flagged(pe)
            if v is None:
                body()
            else:
                with pe.If(v != 0):
                    body()

        @block.scalar
        def _(act):
            def body():
                act.wait_ge(loaded, 16 * LOADS)
                n = 0
                for h in range(HEADS):
                    for c, w in CHUNKS:
                        act.wait_ge(kproj, n + 1)
                        nc.scalar.activation(kh[:, h, c:c + w], psum[0:DK, n % 2, 0:w], ACT.Identity,
                                             bias=bqk[:, 1, h:h + 1]).then_inc(kproj_used, 1)
                        n += 1
                with act.Fori(0, GT) as i:
                    act.wait_ge(q_ps, i + 1)
                    act.wait_ge(q_bias, 1)
                    act.wait_ge(s_used, i * HEADS + HEADS)
                    for h in range(HEADS):
                        last = nc.scalar.activation(qh[:, h, :], psum[0:DK, 6 + h // 4, (h % 4) * GP:(h % 4 + 1) * GP],
                                                    ACT.Identity, bias=bqk[:, 0, h:h + 1], scale=DK ** -0.5)
                    last.then_inc(q_sb, 1)
                    for h in range(HEADS):
                        act.wait_ge(s_ok, i * HEADS + (h + 1))
                        nc.scalar.activation(p_t[:, :], s_t[:, :], ACT.Exp, bias=sm[:, 0:1],
                                             accum_out=sm[:, 1:2]).then_inc(p_ok, 1)
                    act.wait_ge(fT_ps, i + 1)
                    for g in range(3):
                        w = 4 if g < 2 else 2
                        src = psum[:, 3 + g, 0:w * P].rearrange("p (t n) -> p t n", n=P)[:, :, 0:GP]
                        nc.scalar.activation(fT[:, 4 * g:4 * g + w, :], src, ACT.Copy).then_inc(fT_sb, 1)
                    nc.scalar.activation(fT[0:KREM, KT - 1, :], psum[0:KREM, 5, 2 * P:2 * P + GP],
                                         ACT.Copy).then_inc(fT_sb, 1)
                    act.wait_ge(var_ok, i + 1)
                    nc.scalar.activation(sm[:, 5:6], sm[:, 4:5], ACT.Sqrt).then_inc(std_ok, 1)
                with act.Fori(0, GT) as i:
                    act.wait_ge(agg_ps, i + 1)
                    nc.scalar.activation(agg, psum[0:GP, 0, :], ACT.Copy).then_inc(agg_sb, 1)
                    act.wait_ge(aggT_ps, i + 1)
                    act.wait_ge(out_ps, i + 1)
                    src = psum[:, 1, :].rearrange("p (t n) -> p t n", n=P)[:, :, 0:GP]
                    nc.scalar.activation(fT[:, 0:DT, :], src, ACT.Copy).then_inc(aggT_sb, 1)
                    act.wait_ge(out_ps, i + 2)
                    act.wait_ge(y2_out, 16 * i + 16)
                    nc.scalar.activation(z_t[:, :], psum[0:GP, 2, :], ACT.Relu).then_inc(relu_ok, 1)
                    act.wait_ge(var2_ok, i + 1)
                    nc.scalar.activation(sm[:, 5:6], sm[:, 4:5], ACT.Sqrt).then_inc(std2_ok, 1)

            v = flagged(act)
            if v is None:
                body()
            else:
                with act.If(v != 0):
                    body()

        @block.vector
        def _(dve):
            def body():
                step = Steps(chain)

                def link(ins):
                    step.did(ins)
                    step.wait(dve)

                dve.wait_ge(loaded, 16 * LOADS)
                dve.wait_ge(consts, 6)
                nc.vector.tensor_scalar(bqk[:, 0, :], bqk[:, 0, :], DK ** -0.5, None, ALU.mult).then_inc(q_bias, 1)
                link(nc.vector.tensor_copy(pair_f[:, :, :], pair_i[:, :].rearrange("p (c t) -> p t c", t=2)))
                link(nc.vector.tensor_scalar(neg[:, :, :], pair_f[:, :, :], 0.0, float(N), ALU.is_lt, ALU.mult))
                link(nc.vector.tensor_tensor(pair_f[:, :, :], pair_f[:, :, :], neg[:, :, :], ALU.add))
                starts = ((obj_free, 2), (y_ok, 1), (z_ok, 1), (s_used, HEADS), (fT_sb, 4),
                          (y_out, 16), (y2_ok, 1), (out_ps, 1), (y2_out, 16))
                for n, (free, count) in enumerate(starts):
                    nc.vector.memset(token[:, n:n + 1], 0.0).then_inc(free, count)
                before = step.n
                with dve.Fori(0, GT) as i:
                    step.base, step.n = i * PER1, before
                    nc.vector.tensor_tensor(one_sub[:, :, :],
                                            pair_f[:, 0, :].unsqueeze(2).to_broadcast([EP, EC, GP]),
                                            iota16[0:EP, None, 0:GP].to_broadcast([EP, EC, GP]),
                                            ALU.is_equal).then_inc(sub_ready, 1)
                    with dve.Fori(0, EC // 2) as c2:
                        for u in range(2):
                            dve.wait_ge(obj_free, i * EC + c2 * 2 + (u + 1))
                            nc.vector.tensor_scalar(one_obj[:, u, :], iota16[0:EP, :],
                                                    pair_f[:, 1, bass.ds(c2 * 2 + u, 1)], None,
                                                    ALU.is_equal).then_inc(obj_ready, 1)
                    dve.wait_ge(tile_in, 32 * i + 32)
                    link(nc.vector.tensor_scalar(on_diag[:, :], col_row[:, :], 0.0, None, ALU.is_equal))
                    link(nc.vector.tensor_scalar(col_row[:, :], col_row[:, :], -float(GS), None, ALU.add))
                    link(nc.vector.tensor_scalar(a_t[:, :], a_t[:, :], 1.0, None, ALU.is_equal))
                    link(nc.vector.tensor_tensor(a_t[:, :], a_t[:, :], on_diag[:, :], ALU.max))
                    link(nc.vector.tensor_scalar(a_t[:, :], a_t[:, :], -1.0, BIG, ALU.add, ALU.mult))
                    link(nc.vector.scalar_tensor_tensor(a_t[:, :], on_diag[:, :], DIAG, a_t[:, :],
                                                        ALU.mult, ALU.add))
                    dve.wait_ge(em_ps, i + 1)
                    step.did(nc.vector.tensor_scalar(edge[:, :], even[0:GP, :], 1.0, None, ALU.min))
                    step.wait(dve)
                    nc.vector.scalar_tensor_tensor(edge[:, :], on_diag[:, :], 0.5, edge[:, :],
                                                   ALU.is_lt, ALU.mult).then_inc(em_used, 1)
                    dve.wait_ge(em_used, i + 1)
                    for h in range(HEADS):
                        s_bank = even if h % 2 == 0 else odd
                        dve.wait_ge(s_ps, i * HEADS + (h + 1))
                        nc.vector.tensor_tensor(s_t[:, :], s_bank[0:GP, :], edge[:, :], ALU.mult).then_inc(s_used, 1)
                        dve.wait_ge(s_used, i * HEADS + (HEADS + h + 1))
                        link(nc.vector.tensor_tensor(s_t[:, :], s_t[:, :], a_t[:, :], ALU.add))
                        nc.vector.tensor_reduce(sm[:, 0:1], s_t[:, :], AX.X, ALU.max, negate=True).then_inc(s_ok, 1)
                        dve.wait_ge(p_ok, i * HEADS + (h + 1))
                        link(nc.vector.reciprocal(sm[:, 2:3], sm[:, 1:2]))
                        if h == 0:
                            ins = nc.vector.tensor_scalar(f_t[:, :], p_t[:, :], sm[:, 2:3], None, ALU.mult)
                        else:
                            ins = nc.vector.scalar_tensor_tensor(f_t[:, :], p_t[:, :], sm[:, 2:3], f_t[:, :],
                                                                 ALU.mult, ALU.add)
                        link(ins)
                    nc.vector.tensor_scalar(pair_f[:, 0, :], pair_f[:, 0, :], -float(GS), None,
                                            ALU.add).then_inc(f_ok, 1)
                    dve.wait_ge(f_ok, i + 1)
                    dve.wait_ge(o_ps, i + 1)
                    nc.vector.scalar_tensor_tensor(z_t[:, :], psum[0:GP, 0, :], 1.0 / HEADS, xt[:, :],
                                                   ALU.mult, ALU.add).then_inc(z_ok, 1)
                    dve.wait_ge(z_ok, i + 2)
                    link(nc.vector.bn_stats(st[:, :], z_t[:, :]))
                    nc.vector.tensor_copy(sm[:, 7:8], st[:, 0:1])
                    link(nc.vector.bn_aggr(mv[:, :], st[:, :]))
                    nc.vector.tensor_scalar(sm[:, 4:5], mv[:, 1:2], EPS, None, ALU.add).then_inc(var_ok, 1)
                    dve.wait_ge(std_ok, i + 1)
                    link(nc.vector.reciprocal(sm[:, 6:7], sm[:, 5:6]))
                    dve.wait_ge(y_out, 16 * i + 16)
                    nc.vector.tensor_scalar(y_t[:, :], z_t[:, :], mv[:, 0:1], sm[:, 6:7],
                                            ALU.subtract, ALU.mult).then_inc(y_ok, 1)
                    assert step.n - before == PER1, step.n - before
                step = Steps(chain2)
                with dve.Fori(0, GT) as i:
                    step.base, step.n = i * PER2, 0
                    dve.wait_ge(t2_in, 48 * i + 48)
                    dve.wait_ge(relu_ok, i + 1)
                    nc.vector.tensor_tensor(z_t[:, :], z_t[:, :], xt[:, :], ALU.add).then_inc(z2_ok, 1)
                    dve.wait_ge(z2_ok, i + 1)
                    step.did(nc.vector.bn_stats(st[:, :], z_t[:, :]))
                    step.wait(dve)
                    nc.vector.tensor_copy(sm[:, 7:8], st[:, 0:1])
                    step.did(nc.vector.bn_aggr(mv[:, :], st[:, :]))
                    step.wait(dve)
                    nc.vector.tensor_scalar(sm[:, 4:5], mv[:, 1:2], EPS, None, ALU.add).then_inc(var2_ok, 1)
                    dve.wait_ge(std2_ok, i + 1)
                    step.did(nc.vector.reciprocal(sm[:, 6:7], sm[:, 5:6]))
                    step.wait(dve)
                    dve.wait_ge(y2_out, 16 * i + 16)
                    nc.vector.tensor_scalar(y_t[:, :], z_t[:, :], mv[:, 0:1], sm[:, 6:7],
                                            ALU.subtract, ALU.mult).then_inc(y2_ok, 1)
                    assert step.n == PER2, step.n

            v = flagged(dve)
            if v is None:
                body()
            else:
                with dve.If(v != 0):
                    body()


PER1 = 7 + 3 * HEADS + 3
PER2 = 3


def fast_path(nc, flag, x, adj, adjT, diag, pairs, wqT, bq, wkT, bk, wT, b, const32, const16, zrows, out):
    ctx = ExitStack()
    with ctx:
        def sb(name, shape, dt=F32):
            return ctx.enter_context(nc.sbuf_tensor("f_" + name, shape, dt))

        def sem(name):
            return ctx.enter_context(nc.semaphore("f_" + name))

        stage = sb("stage", [P, STAGES * N])
        adj32 = [stage[:, s * N:(s + 1) * N] for s in range(STAGES)]
        wqk = stage[:, 0:2 * DT * D].rearrange("p (w t n) -> p w t n", w=2, t=DT)
        a16 = sb("a16", [P, KT, N], F16)
        x_agg = sb("x_agg", [P, KT * D])
        x32 = x_agg[:, :].rearrange("p (t n) -> p t n", n=D)
        agg16 = x_agg[:, 0:DT * N].bitcast(F16).rearrange("p (h t n) -> p h t n", h=2, t=DT)
        x_slots = sb("x_slots", [P, KT * D])
        x16 = x_slots[:, :].bitcast(F16).rearrange("p (h t n) -> p h t n", h=2, n=D)
        x2 = sb("x2", [P, KT, D])
        x216 = sb("x216", [P, 2, KT, D], F16)
        warm = x216[:, 1, KT - 1, :]
        w16 = sb("w16", [P, 2, DT, D], F16)
        shared = sb("shared", [P, EC * HALF // 2])
        w32 = shared[:, 0:DT * D].rearrange("p (t n) -> p t n", n=D)
        one_slot = shared[0:EP, 0:EC * HALF // 2].bitcast(F16).rearrange("p (c s) -> p c s", s=HALF)
        a_col = shared[:, 0:N]
        square = sb("square", [P, N])
        tx = sb("tx", [P, 2, D])
        a_sum = tx[:, :, :].rearrange("p a n -> p (a n)").bitcast(F16)[:, 0:N]
        z = sb("z", [P, ZB, ZW])
        st = sb("st", [P, 4, 6])
        nb = sb("nb", [P, 4])
        before = sb("before", [P, 1])
        sd = sb("sd", [P, 4])
        rs = sb("rs", [P, 4])
        deg = sb("deg", [P, KT])
        cb = sb("cb", [P, KT])
        gb = sb("gb", [P, KT])
        rzb = sb("rzb", [P, KT])
        eps26 = sb("eps26", [P, 1])
        eps1 = sb("eps1", [P, 1])
        half = sb("half", [P, 1])
        quarter = sb("quarter", [P, 1])
        one1 = sb("one1", [P, 1])
        epsy = sb("epsy", [P, 1])
        ste = sb("ste", [P, 6])
        mve = sb("mve", [P, 2])
        sde = sb("sde", [P, 1])
        rse = sb("rse", [P, 1])
        adj_off = sb("adj_off", [P, KT])
        x_sq = sb("x_sq", [P, KT])
        seen = sb("seen", [P, 7])
        limit = sb("limit", [P, 7])
        kept = sb("kept", [P, 7])
        kept1 = sb("kept1", [P, 1])
        kept16 = sb("kept16", [P, 1], F16)
        diag_sb = sb("diag_sb", [2, N // 2])
        pair_i = sb("pair_i", [EP, 2 * EC], I32)
        pair_f = sb("pair_f", [EP, 2, EC])
        tmp_e = sb("tmp_e", [EP, 2, EC])
        valid = sb("valid", [EP, EC])
        look_f = sb("look_f", [EP, EC])
        look_i = sb("look_i", [EP, EC], I32)
        looked = sb("looked", [EP, EC])
        vals = sb("vals", [EP, EC, 3], F16)
        active = sb("active", [EP, EC])
        upto = sb("upto", [EP, EC])
        zero_e = sb("zero_e", [EP, EC])
        total16 = sb("total16", [EP, 1], F16)
        pos = sb("pos", [EP, EC])
        pos16 = sb("pos16", [EP, EC], F16)
        slot = sb("slot", [P, 3])
        slot_i = sb("slot_i", [P, 2], I32)
        node = sb("node", [P, 1])
        spread = sb("spread", [HALF, 3, P], F16)
        slot16 = sb("slot16", [HALF, 3], F16)
        across = sb("across", [P, 3, P])
        rowm = sb("rowm", [P, P])
        pairm = sb("pairm", [P, HALF])
        junk = sb("junk", [P, HALF])
        rowoff = sb("rowoff", [P, HALF])
        later = sb("later", [P, 2])
        ul = sb("ul", [P, 2])
        used32 = sb("used32", [P, 1])
        xs = sb("xs", [P, D])
        xo = sb("xo", [P, D])
        bqk = sb("bqk", [P, 2, DT])
        mx = sb("mx", [P, HEADS])
        arg = sb("arg", [P, 3, HEADS])
        ex = sb("ex", [P, 3, HEADS])
        exu = sb("exu", [P, HEADS + 1])
        nn = sb("nn", [P, 1])
        zz = sb("zz", [P, HEADS])
        cdw = sb("cdw", [P, 3])
        sm = sb("sm", [P, 8])
        ac16 = sb("ac16", [P, N], F16)
        bt = sb("bt", [P, D])
        ones1 = sb("ones1", [P, 1], F16)
        zs = sb("zs", [P, ZW])
        ze = sb("ze", [P, 2, D])
        vv = ze[:, 0, :]
        psum = ctx.enter_context(nc.psum_tensor("f_psum", [P, 8, 512], F32))

        def at(place, first, *dims):
            size = 1
            for n in dims:
                size *= n
            flat = place[:, first:first + size]
            return flat if len(dims) == 1 else flat.rearrange("p (a b) -> p a b", b=dims[1])

        xsoT = at(x_slots, 0, 8, HALF)
        kb = at(x_slots, 512, DT, HALF)
        qk = at(x_slots, 768, DT, HALF)
        sT = at(x_slots, 1024, HEADS, HALF)
        sI = at(x_slots, 1536, HEADS, HALF)
        txe = at(x_slots, 2048, D)
        xoc = x_slots[0:HALF, 2560:2560 + D]
        d16 = at(x_slots, 3072, D // 2).bitcast(F16)
        v16 = at(x_slots, 3328, D // 2).bitcast(F16)
        r_sb = at(x_slots, 3584, 3, D)
        delta = tx[:, 0, :]
        hi_tmp = tx[:, 1, :].bitcast(F16).rearrange("p (a n) -> p a n", n=D)
        dT16 = square[:, 512:1024].bitcast(F16).rearrange("p (h t n) -> p h t n", h=2, n=P)
        y = at(stage, 0, 3, D)

        c32 = sb("c32", [P, C32])
        c16 = sb("c16", [P, C16], F16)
        ident, same = c32[:, 0:P], c32[:, P:P + HALF]
        lower = c32[:, P + HALF:2 * P]
        hsel = c32[:, 2 * P:4 * P].rearrange("p (a n) -> p a n", n=P)
        last32 = c32[:, 4 * P:4 * P + 1]
        iota16, ones16 = c16[:, 0:N], c16[:, N:N + P]
        tri = c16[0:EP, N + P:N + P + EP]
        cap = c16[0:EP, N + P + EP:N + P + EP + HALF]
        twice16 = c16[0:HALF, N + P + EP + HALF:C16]
        oh16 = iota16

        pairs_in = sem("pairs_in")
        x_in = [sem(f"x_in{k}") for k in range(KT)]
        adj_in = [sem(f"adj_in{s}") for s in range(STAGES)]
        adj_first_in = [sem(f"adj_first_in{n}") for n in range(2)]
        w_in = sem("w_in")
        small_in = sem("small_in")
        bt_in = sem("bt_in")
        wqk_in = sem("wqk_in")
        x2_fixed = sem("x2_fixed")
        bt_zero = sem("bt_zero")
        looked_in = [sem(f"looked_in{n}") for n in range(len(BATCHES))]
        xs_in, xo_in = sem("xs_in"), sem("xo_in")
        zs_in, acol_in = sem("zs_in"), sem("acol_in")
        act_chain = sem("act_chain")
        x_hi = sem("x_hi")
        adj_checked = sem("adj_checked")
        a16_first = sem("a16_first")
        tx_ok = sem("tx_ok")
        sd_ok = sem("sd_ok")
        x2_hi = sem("x2_hi")
        agg_hi = sem("agg_hi")
        w_hi = sem("w_hi")
        checks = sem("checks")
        xsoT_ok = sem("xsoT_ok")
        kb_ok = sem("kb_ok")
        ex_ok = sem("ex_ok")
        txe_ok = sem("txe_ok")
        sde_ok = sem("sde_ok")
        dT_hi = sem("dT_hi")
        vsq_ok = sem("vsq_ok")
        sd2_ok = sem("sd2_ok")
        chain = sem("chain")
        look_ok = sem("look_ok")
        a16_ok = sem("a16_ok")
        sum_ok = sem("sum_ok")
        x_lo = sem("x_lo")
        w_lo = sem("w_lo")
        z_ok = sem("z_ok")
        var_ok = sem("var_ok")
        x2_ok = sem("x2_ok")
        x2_lo = sem("x2_lo")
        agg_lo = sem("agg_lo")
        coef_ok = sem("coef_ok")
        total_ok = sem("total_ok")
        one_ok = sem("one_ok")
        slot_ok = sem("slot_ok")
        index_ok = sem("index_ok")
        rowm_ok = sem("rowm_ok")
        ac_ok = sem("ac_ok")
        oh_ok = sem("oh_ok")
        qk_ok = sem("qk_ok")
        arg_ok = sem("arg_ok")
        exu_ok = sem("exu_ok")
        coefe_ok = sem("coefe_ok")
        xoc_ok = sem("xoc_ok")
        ze_ok = sem("ze_ok")
        delta_ok = sem("delta_ok")
        d16_ok = sem("d16_ok")
        dT_lo = sem("dT_lo")
        v_ok = sem("v_ok")
        v16_ok = sem("v16_ok")
        kept_ok = sem("kept_ok")
        flag_ok = sem("flag_ok")
        small_ok = sem("small_ok")
        ones_ok = sem("ones_ok")
        sT_used = sem("sT_used")
        y_used = sem("y_used")
        var2_ok = sem("var2_ok")
        y_ok = sem("y_ok")
        l0_ps = sem("l0_ps")
        deg_ps = sem("deg_ps")
        agg_ps = sem("agg_ps")
        off_ps = sem("off_ps")
        slot_ps = sem("slot_ps")
        across_ps = sem("across_ps")
        xsoT_ps = sem("xsoT_ps")
        qk_ps = sem("qk_ps")
        sT_ps = sem("sT_ps")
        zz_ps = sem("zz_ps")
        corr_ps = sem("corr_ps")
        dT_ps = sem("dT_ps")
        dw_ps = sem("dw_ps")
        kept_ps = sem("kept_ps")
        y_ps = sem("y_ps")
        r_ps = sem("r_ps")
        const_in = sem("const_in")
        zrow_ok = sem("zrow_ok")
        zrow_out = [sem(f"zrow_out{s}") for s in range(ZB)]
        r_copied = sem("r_copied")
        bias_ok = sem("bias_ok")
        out_done = [sem(f"out_done{s}") for s in range(3)]

        L0_BANK = [0, 1, 2, 3, 4, 5, 7, 0, 1, 2, 3]
        DEG_BANK = 6
        A_BANK = [4, 5, 6, 7, 0, 1]
        BLOCKS = [(2 * r + d, c) for r in range(2) for c in range(3) for d in range(2)]
        Y_BANK = [A_BANK[i % 6] for i in range(KT)]
        R_BANK = [2 + i % 2 for i in range(KT)]
        PARTS = [(0, D // 2), (D // 2, D)]
        PART_BANK = [A_BANK[(KT - 1 + n) % 6] for n in range(2)]

        block = ctx.enter_context(nc.Block())

        @block.sync
        def _(sp):
            sp.dma_start(pair_i[:, :], pairs.rearrange("(p c) t -> p (c t)", p=EP)).then_inc(pairs_in, 16)
            for k in range(KT):
                r = krows(k)
                sp.dma_start(x32[0:r, k, :], x[k * P:k * P + r, :]).then_inc(x_in[k], 16)
                if k >= STAGES:
                    sp.wait_ge(a16_ok, k - STAGES + 1)
                    sp.wait_ge(adj_checked, k - STAGES + 1)
                if k == 0:
                    for n, (c0, c1) in enumerate(FIRST):
                        sp.dma_start(adj32[0][:, c0:c1], adjT[0:P, c0:c1]).then_inc(adj_first_in[n], 16)
                    sp.dma_start(adj32[0][:, G1 * P:N], adjT[0:P, G1 * P:N]).then_inc(adj_in[0], 16)
                else:
                    sp.dma_start(adj32[k % STAGES][0:r, :], adjT[k * P:k * P + r, :]).then_inc(adj_in[k % STAGES], 16)
            sp.dma_start(w32, wT.rearrange("(t p) n -> p t n", p=P)).then_inc(w_in, 16)
            sp.dma_start(c32[:, :], const32).then_inc(const_in, 16)
            sp.dma_start(c16[:, :], const16).then_inc(const_in, 16)
            sp.wait_ge(bt_zero, 1)
            for s in (SLOTS, HALF + SLOTS):
                sp.dma_start(bt[s:s + 1, :], b.rearrange("(o n) -> o n", o=1)).then_inc(bt_in, 16)
            with nc.allow_non_contiguous_dma(reason="small vectors"):
                sp.dma_start(bqk[:, 0, :], bq.rearrange("(t p) -> p t", p=P)).then_inc(small_in, 16)
                sp.dma_start(bqk[:, 1, :], bk.rearrange("(t p) -> p t", p=P)).then_inc(small_in, 16)
            sp.dma_start(diag_sb[:, :], diag.rearrange("(p n) -> p n", p=2)).then_inc(small_in, 16)
            for i in range(KT):
                r = krows(i)
                sp.wait_ge(zrow_ok, i + 1)
                sp.dma_start(zrows[i * P:i * P + r, :], z[0:r, i % ZB, :]).then_inc(zrow_out[i % ZB], 16)
            sp.wait_ge(a16_ok, KT)
            sp.wait_ge(adj_checked, KT)
            sp.dma_start(wqk[:, 0, :, :], wqT.rearrange("(t p) n -> p t n", p=P)).then_inc(wqk_in, 16)
            sp.dma_start(wqk[:, 1, :, :], wkT.rearrange("(t p) n -> p t n", p=P)).then_inc(wqk_in, 16)
            for i in range(KT):
                r = krows(i)
                if i < KT - 1:
                    sp.wait_ge(y_ok, i + 1)
                else:
                    sp.wait_ge(bias_ok, KT)
                sp.dma_start(out[i * P:i * P + r, :], y[0:r, i % 3, :]).then_inc(out_done[i % 3], 16)
            for s in range(3):
                sp.wait_ge(out_done[s], 16 * len(range(s, KT, 3)))

        @block.gpsimd
        def _(pool):
            g = nc.gpsimd
            g.memset(bt[:, :], 0.0).then_inc(bt_zero, 1)
            pool.wait_ge(look_ok, 1)
            for n, (c0, c1) in enumerate(BATCHES):
                for c in range(c0, c1):
                    g.indirect_dma_start(looked[:, c:c + 1], None,
                                         adj.rearrange("a (b o) -> (a b) o", o=1),
                                         bass.IndirectOffsetOnAxis(look_i[:, c:c + 1], 0)).then_inc(looked_in[n], 16)
            pool.wait_ge(index_ok, 1)
            pool.wait_ge(slot_ps, 1)

            def rows(dst, src, which, done):
                g.indirect_dma_start(dst, None, src,
                                     bass.IndirectOffsetOnAxis(slot_i[:, which:which + 1], 0)).then_inc(done, 16)

            rows(xs[:, :], x, 0, xs_in)
            rows(xo[:, :], x, 1, xo_in)
            for s in range(ZB):
                pool.wait_ge(zrow_out[s], 16 * len(range(s, KT, ZB)))
            rows(zs[:, :], zrows, 0, zs_in)
            rows(a_col, adjT, 0, acol_in)
            for i in range(KT):
                r = krows(i)
                pool.wait_ge(r_copied, i + 1)
                g.tensor_tensor(x2[0:r, i, :], x2[0:r, i, :], r_sb[0:r, i % 3, :], ALU.add).then_inc(x2_fixed, 1)

        @block.scalar
        def _(act):
            s = nc.scalar
            did = Steps(act_chain)

            def link(ins):
                did.did(ins)
                did.wait(act)

            act.wait_ge(small_ok, 1)
            did.did(s.activation(sd[:, 0:1], half[:, :], ACT.Square))

            act.wait_ge(x_in[0], 16)
            s.activation(x16[:, 0, 0, :], x32[:, 0, :], ACT.Identity, scale=XS).then_inc(x_hi, 1)
            for n, (c0, c1) in enumerate(FIRST):
                act.wait_ge(adj_first_in[n], 16)
                s.activation(a16[:, 0, c0:c1], adj32[0][:, c0:c1], ACT.Identity).then_inc(a16_first, 1)
            act.wait_ge(small_ok, 2)

            def check_adj(k):
                r = krows(k)
                act.wait_ge(adj_in[k % STAGES], 16 * (k // STAGES + 1))
                if k:
                    act.wait_ge(adj_checked, k)
                link(s.activation(square[0:r, :], adj32[k % STAGES][0:r, :], ACT.Square, bias=half[0:r, :]))
                s.activation(square[0:r, :], square[0:r, :], ACT.Square, bias=quarter[0:r, :],
                             accum_out=adj_off[0:r, k:k + 1]).then_inc(adj_checked, 1)

            for k in range(KT - STAGES):
                check_adj(k)
            act.wait_ge(w_in, 16)
            s.activation(w16[:, 0, :, :], w32, ACT.Identity, scale=WS).then_inc(w_hi, 1)
            act.wait_ge(w_hi, 1)
            act.wait_ge(adj_checked, KT - STAGES)
            s.activation(square[:, :].bitcast(F16)[:, 0:DT * D], w16[:, 0, :, :].rearrange("p t n -> p (t n)"),
                         ACT.Square, accum_out=seen[:, 2:3]).then_inc(checks, 1)
            act.wait_ge(checks, 1)
            act.wait_ge(coef_ok, 2)

            def share(i):
                r = krows(i)
                if i >= 2:
                    act.wait_ge(z_ok, i - 1)
                s.activation(tx[0:r, i % 2, :], x32[0:r, i, :], ACT.Identity, scale=gb[0:r, i:i + 1]).then_inc(tx_ok, 1)

            def root(i):
                r = krows(i)
                act.wait_ge(var_ok, i + 1)
                s.activation(sd[0:r, i % 4:i % 4 + 1], z[0:r, i % ZB, ZVAR:ZVAR + 1], ACT.Sqrt, bias=eps26[0:r, :],
                             scale=1.0 / YS ** 2).then_inc(sd_ok, 1)

            def high(i):
                r = krows(i)
                act.wait_ge(x2_ok, i + 1)
                s.activation(x216[0:r, 0, i, :], x2[0:r, i, :], ACT.Identity, scale=XS / YS).then_inc(x2_hi, 1)

            share(0)
            for i in range(KT):
                if i + 1 < KT:
                    share(i + 1)
                root(i)
                if i >= 1:
                    high(i - 1)
                r = krows(i)
                link(s.activation(square[0:r, 0:D], x32[0:r, i, :], ACT.Square, accum_out=x_sq[0:r, i:i + 1]))
            high(KT - 1)
            for k in range(KT - STAGES, KT):
                check_adj(k)
            act.wait_ge(adj_checked, KT)
            act.wait_ge(small_in, 48)
            link(s.activation(square[0:2, 0:N // 2], diag_sb[:, :], ACT.Square, bias=one1[0:2, :],
                              accum_out=seen[0:2, 6:7]))

            def agg_high(n):
                t, c = BLOCKS[n]
                c0, w = CHUNKS[c]
                act.wait_ge(agg_ps, n + 1)
                if n == 0:
                    did.wait(act)
                s.activation(agg16[:, 0, t, c0:c0 + w], psum[:, A_BANK[n % 6], 0:w], ACT.Identity,
                             scale=AS / XS).then_inc(agg_hi, 1)

            def edge_xT():
                act.wait_ge(xsoT_ps, 1)
                s.activation(xsoT[:, :, :], psum[:, 3, :].rearrange("p (t n) -> p t n", n=HALF),
                             ACT.Identity).then_inc(xsoT_ok, 1)

            def edge_k():
                act.wait_ge(qk_ps, 1)
                for t in range(DT):
                    last = s.activation(kb[:, t, :], psum[:, 2, 256 + t * HALF:256 + (t + 1) * HALF], ACT.Identity,
                                        bias=bqk[:, 1, t:t + 1])
                last.then_inc(kb_ok, 1)

            def edge_exp():
                act.wait_ge(arg_ok, 1)
                s.activation(ex[:, :, :], arg[:, :, :], ACT.Exp).then_inc(ex_ok, 1)

            def edge_share():
                act.wait_ge(coefe_ok, 1)
                s.activation(txe[:, :], xs[:, :], ACT.Identity, scale=sm[:, 3:4]).then_inc(txe_ok, 1)

            def edge_root():
                act.wait_ge(ze_ok, 1)
                s.activation(sde[:, :], mve[:, 1:2], ACT.Sqrt, bias=eps1[:, :],
                             scale=1.0 / XS ** 2).then_inc(sde_ok, 1)

            def edge_dT():
                act.wait_ge(dT_ps, 1)
                s.activation(dT16[:, 0, :, :], psum[:, 2, :].rearrange("p (t n) -> p t n", n=P),
                             ACT.Identity).then_inc(dT_hi, 1)

            def edge_v():
                act.wait_ge(v_ok, 1)
                s.activation(square[:, 0:D], vv[:, :], ACT.Square, accum_out=seen[:, 5:6]).then_inc(vsq_ok, 1)

            def root2(i):
                r = krows(i)
                act.wait_ge(var2_ok, i + 1)
                s.activation(sd[0:r, i % 4:i % 4 + 1], z[0:r, i % ZB, ZVAR:ZVAR + 1], ACT.Sqrt,
                             bias=epsy[0:r, :]).then_inc(sd2_ok, 1)

            def copy_r(i):
                r = krows(i)
                act.wait_ge(r_ps, i + 1)
                if i >= 3:
                    act.wait_ge(x2_fixed, i - 2)
                s.activation(r_sb[0:r, i % 3, :], psum[0:r, R_BANK[i], :], ACT.Identity).then_inc(r_copied, 1)

            def normal(i):
                r = krows(i)
                act.wait_ge(bias_ok, i + 1)
                if i >= 3:
                    act.wait_ge(out_done[i % 3], 16 * (i // 3))
                s.activation(y[0:r, i % 3, :], z[0:r, i % ZB, 0:D], ACT.Identity, scale=rs[0:r, i % 4:i % 4 + 1],
                             bias=nb[0:r, i % 4:i % 4 + 1]).then_inc(y_ok, 1)

            for n in range(7):
                agg_high(n)
            edge_xT()
            agg_high(7)
            edge_k()
            agg_high(8)
            edge_exp()
            agg_high(9)
            edge_share()
            edge_root()
            agg_high(10)
            agg_high(11)
            edge_dT()
            copy_r(0)
            copy_r(1)
            edge_v()
            for i in range(KT):
                if i + 2 < KT:
                    copy_r(i + 2)
                root2(i)
                if i >= 1:
                    normal(i - 1)

        @block.vector
        def _(dve):
            v = nc.vector
            did = Steps(chain)

            def link(ins):
                did.did(ins)
                did.wait(dve)

            v.memset(half[:, :], -0.5).then_inc(small_ok, 1)
            v.memset(warm, 0.0).then_inc(ones_ok, 1)
            v.memset(ones1[:, :], 1.0).then_inc(ones_ok, 1)
            for t, value in ((quarter, -0.25), (one1, -1.0), (eps26, EPS * (XS / YS) ** 2),
                             (eps1, EPS), (epsy, EPS * YS ** 2), (adj_off, 0.0), (x_sq, 0.0), (seen, 0.0),
                             (deg, 0.0)):
                did.did(v.memset(t[:, :], value))
            for n, top in enumerate((0.0, X_SQ_MAX, W_SQ_MAX * WS ** 2, DEG_MAX, float(SLOTS), V_SQ_MAX, 0.0)):
                did.did(v.memset(limit[:, n:n + 1], top))
            did.did(v.memset(zero_e[:, :], 0.0))
            v.memset(vals[:, :, 2:3], 1.0).then_inc(small_ok, 1)

            def high_x(k):
                r = krows(k)
                dve.wait_ge(x_in[k], 16)
                v.tensor_scalar(x16[0:r, 0, k, :], x32[0:r, k, :], XS, None, ALU.mult).then_inc(x_hi, 1)

            def low_x(k):
                r = krows(k)
                dve.wait_ge(x_hi, k + 1)
                v.scalar_tensor_tensor(x16[0:r, 1, k, :], x32[0:r, k, :], XS, x16[0:r, 0, k, :],
                                       ALU.mult, ALU.subtract).then_inc(x_lo, 1)

            dve.wait_ge(pairs_in, 16)
            link(v.tensor_copy(pair_f[:, :, :], pair_i[:, :].rearrange("p (c t) -> p t c", t=2)))
            link(v.tensor_scalar(tmp_e[:, :, :], pair_f[:, :, :], 0.0, float(N), ALU.is_lt, ALU.mult))
            link(v.tensor_tensor(pair_f[:, :, :], pair_f[:, :, :], tmp_e[:, :, :], ALU.add))
            link(v.tensor_scalar(tmp_e[:, :, :], pair_f[:, :, :], 0.0, float(N - 1), ALU.max, ALU.min))
            link(v.scalar_tensor_tensor(look_f[:, :], tmp_e[:, 0, :], float(N), tmp_e[:, 1, :], ALU.mult, ALU.add))
            v.tensor_copy(look_i[:, :], look_f[:, :]).then_inc(look_ok, 1)
            low_x(0)
            link(v.tensor_scalar(tmp_e[:, :, :], pair_f[:, :, :], 0.0, None, ALU.is_ge))
            link(v.scalar_tensor_tensor(tmp_e[:, :, :], pair_f[:, :, :], float(N), tmp_e[:, :, :], ALU.is_lt, ALU.mult))
            link(v.tensor_tensor(valid[:, :], pair_f[:, 0, :], pair_f[:, 1, :], ALU.not_equal))
            link(v.tensor_tensor(valid[:, :], valid[:, :], tmp_e[:, 0, :], ALU.mult))
            link(v.tensor_tensor(valid[:, :], valid[:, :], tmp_e[:, 1, :], ALU.mult))
            link(v.tensor_tensor(pair_f[:, :, :], pair_f[:, :, :], valid[:, None, :].to_broadcast([EP, 2, EC]), ALU.mult))
            did.did(v.tensor_copy(vals[:, :, 0:2].rearrange("p c t -> p t c"), pair_f[:, :, :]))

            def sum_adj(k):
                r = krows(k)
                dve.wait_ge(a16_ok, k + 1)
                if k == 1:
                    dve.wait_ge(a16_first, len(FIRST))
                else:
                    dve.wait_ge(sum_ok, k - 1)
                v.tensor_tensor(a_sum[0:r, :], a16[0:r, 0, :] if k == 1 else a_sum[0:r, :], a16[0:r, k, :],
                                ALU.add).then_inc(sum_ok, 1)

            for k in range(KT):
                r = krows(k)
                if k >= 1:
                    high_x(k)
                if k >= 2:
                    sum_adj(k - 1)
                if k >= 1:
                    low_x(k)
                dve.wait_ge(adj_in[k % STAGES], 16 * (k // STAGES + 1))
                c0 = G1 * P if k == 0 else 0
                v.tensor_copy(a16[0:r, k, c0:N], adj32[k % STAGES][0:r, c0:N]).then_inc(a16_ok, 1)
            sum_adj(KT - 1)

            dve.wait_ge(deg_ps, 1)
            for rows, cols in ((P, slice(0, KT - 1)), (KREM, slice(KT - 1, KT))):
                src = psum[0:rows, DEG_BANK, cols]
                did.did(v.tensor_copy(deg[0:rows, cols], src))
                link(v.tensor_scalar(rzb[0:rows, cols], src, ALPHA, ALPHA1, ALU.mult, ALU.add))
                link(v.reciprocal(rzb[0:rows, cols], rzb[0:rows, cols]))
                did.did(v.tensor_scalar(cb[0:rows, cols], rzb[0:rows, cols], ALPHA, None, ALU.mult))
                v.tensor_scalar(gb[0:rows, cols], rzb[0:rows, cols], XS * ALPHA1, XS,
                                ALU.mult, ALU.add).then_inc(coef_ok, 1)

            def statistics(rows, i, ready, mark):
                dve.wait_ge(*mark)
                did.did(v.bn_stats(st[0:rows, i % 4, :], z[0:rows, i % ZB, 0:D]))
                did.wait(dve)
                v.bn_aggr(z[0:rows, i % ZB, ZMEAN:ZVAR + 1], st[0:rows, i % 4, :]).then_inc(ready, 1)

            def finish(i):
                r = krows(i)
                dve.wait_ge(sd_ok, i + 1)
                v.reciprocal(z[0:r, i % ZB, ZROOT:ZROOT + 1], sd[0:r, i % 4:i % 4 + 1]).then_inc(zrow_ok, 1)
                dve.wait_ge(zrow_ok, i + 1)
                v.tensor_scalar(x2[0:r, i, :], z[0:r, i % ZB, 0:D], z[0:r, i % ZB, ZMEAN:ZMEAN + 1],
                                z[0:r, i % ZB, ZROOT:ZROOT + 1], ALU.subtract, ALU.mult).then_inc(x2_ok, 1)

            def low(i):
                r = krows(i)
                dve.wait_ge(x2_hi, i + 1)
                v.scalar_tensor_tensor(x216[0:r, 1, i, :], x2[0:r, i, :], XS / YS, x216[0:r, 0, i, :],
                                       ALU.mult, ALU.subtract).then_inc(x2_lo, 1)

            def count(n):
                c0, c1 = BATCHES[n]
                dve.wait_ge(looked_in[n], 16 * (c1 - c0))
                link(v.scalar_tensor_tensor(active[:, c0:c1], looked[:, c0:c1], 1.0, valid[:, c0:c1], ALU.is_equal, ALU.mult))
                link(v.tensor_tensor_scan(upto[:, c0:c1], active[:, c0:c1], zero_e[:, c0:c1], before[0:EP, 0:1],
                                          ALU.add, ALU.add))
                v.tensor_tensor(total16[:, :], upto[:, c1 - 1:c1], before[0:EP, :], ALU.subtract).then_inc(total_ok, 1)

            dve.wait_ge(coef_ok, 2)
            for i in range(KT):
                r = krows(i)
                dve.wait_ge(l0_ps, i + 1)
                dve.wait_ge(tx_ok, i + 1)
                if i >= ZB:
                    dve.wait_ge(zrow_out[i % ZB], 16 * (i // ZB))
                did.did(v.tensor_copy(z[0:r, i % ZB, ZDEG:ZDEG + 1], deg[0:r, i:i + 1]))
                v.scalar_tensor_tensor(z[0:r, i % ZB, 0:D], psum[0:r, L0_BANK[i], :], cb[0:r, i:i + 1], tx[0:r, i % 2, :],
                                       ALU.mult, ALU.add).then_inc(z_ok, 1)
                statistics(r, i, var_ok, (z_ok, i + 1))
                if i >= 1:
                    finish(i - 1)
                if i >= 2:
                    low(i - 2)
            finish(KT - 1)
            low(KT - 2)
            low(KT - 1)
            dve.wait_ge(const_in, 32)
            did.did(v.memset(before[:, :], 0.0))
            count(0)
            dve.wait_ge(w_hi, 1)
            v.scalar_tensor_tensor(w16[:, 1, :, :].rearrange("p t n -> p (t n)"), w32.rearrange("p t n -> p (t n)"), WS,
                                   w16[:, 0, :, :].rearrange("p t n -> p (t n)"), ALU.mult, ALU.subtract).then_inc(w_lo, 1)
            dve.wait_ge(bt_in, 32)
            link(v.tensor_scalar(bt[:, :], bt[:, :], WS, None, ALU.mult))

            def agg_low(n):
                t, c = BLOCKS[n]
                c0, w = CHUNKS[c]
                dve.wait_ge(agg_hi, n + 1)
                v.scalar_tensor_tensor(agg16[:, 1, t, c0:c0 + w], psum[:, A_BANK[n % 6], 0:w], AS / XS,
                                       agg16[:, 0, t, c0:c0 + w], ALU.mult, ALU.subtract).then_inc(agg_lo, 1)

            def number(n):
                c0, c1 = BATCHES[n]
                w = c1 - c0
                dve.wait_ge(off_ps, n + 1)
                did.did(v.tensor_tensor(before[:, :], before[:, :], psum[:, 2, 1:2], ALU.add))
                link(v.scalar_tensor_tensor(pos[:, c0:c1], upto[:, c0:c1], psum[0:EP, 2, 0:1], active[:, c0:c1],
                                            ALU.add, ALU.mult))
                link(v.tensor_scalar(pos16[:, c0:c1], pos[:, c0:c1], 100.0, None, ALU.min))
                v.tensor_tensor(one_slot[:, c0:c1, :], pos16[:, c0:c1].unsqueeze(2).to_broadcast([EP, w, HALF]),
                                cap[:, None, :].to_broadcast([EP, w, HALF]), ALU.is_equal).then_inc(one_ok, 1)

            number(0)
            agg_low(0)
            count(1)
            agg_low(1)
            number(1)
            count(2)
            agg_low(2)
            number(2)
            agg_low(3)
            agg_low(4)
            agg_low(5)
            dve.wait_ge(slot_ps, 1)
            link(v.tensor_copy(slot16[:, :], psum[0:HALF, 3, 0:3]))
            v.tensor_tensor(spread[:, :, :], slot16[:, :].unsqueeze(2).to_broadcast([HALF, 3, P]),
                            twice16[:, None, :].to_broadcast([HALF, 3, P]), ALU.mult).then_inc(slot_ok, 1)
            dve.wait_ge(across_ps, 1)
            link(v.tensor_copy(slot[:, :], psum[:, 2, 384:387]))
            v.tensor_copy(slot_i[:, :], slot[:, 0:2]).then_inc(index_ok, 1)
            did.did(v.scalar_tensor_tensor(node[:, :], slot[:, 0:1], -1.0, slot[:, 2:3], ALU.add, ALU.add))
            link(v.tensor_copy(across[:, :, :], psum[:, 2, 0:384].rearrange("p (t s) -> p t s", s=P)))
            v.scalar_tensor_tensor(rowm[:, :], across[:, 0, :], node[:, 0:1], across[:, 2, :],
                                   ALU.is_equal, ALU.mult).then_inc(rowm_ok, 1)
            dve.wait_ge(rowm_ok, 1)
            link(v.scalar_tensor_tensor(pairm[:, :], across[:, 1, 0:HALF], slot[:, 1:2], rowm[:, 0:HALF],
                                        ALU.is_equal, ALU.mult))
            agg_low(6)
            did.did(v.tensor_scalar(rowoff[:, :], rowm[:, 0:HALF], -1.0, BIG, ALU.add, ALU.mult))
            link(v.tensor_tensor(pairm[:, :], pairm[:, :], lower[:, :], ALU.mult))
            did.did(v.tensor_reduce(later[:, 0:1], pairm[:, :], AX.X, ALU.max))
            link(v.tensor_tensor(junk[:, :], rowm[:, 0:HALF], lower[:, :], ALU.mult))
            link(v.tensor_reduce(later[:, 1:2], junk[:, :], AX.X, ALU.max))
            link(v.tensor_scalar(ul[:, :], later[:, :], -1.0, 1.0, ALU.mult, ALU.add))
            link(v.tensor_scalar(ul[:, :], ul[:, :], slot[:, 2:3], None, ALU.mult))
            did.did(v.tensor_copy(exu[:, HEADS:HEADS + 1], ul[:, 0:1]))
            link(v.tensor_scalar(used32[:, :], slot[:, 2:3], AS, None, ALU.mult))
            v.tensor_scalar(oh16, iota16, node[:, 0:1], YS / XS, ALU.is_equal, ALU.mult).then_inc(oh_ok, 1)
            dve.wait_ge(zs_in, 16)
            link(v.tensor_scalar(sm[:, 4:5], zs[:, ZDEG:ZDEG + 1], ALPHA, ALPHA1, ALU.mult, ALU.add))
            link(v.reciprocal(sm[:, 5:6], sm[:, 4:5]))
            did.did(v.tensor_scalar(sm[:, 6:7], sm[:, 5:6], XS * ALPHA1, XS, ALU.mult, ALU.add))
            link(v.tensor_scalar(sm[:, 7:8], zs[:, ZROOT:ZROOT + 1], ul[:, 1:2], XS / YS, ALU.mult, ALU.mult))
            did.did(v.tensor_scalar(ze[:, 1, :], zs[:, 0:D], zs[:, ZMEAN:ZMEAN + 1], sm[:, 7:8], ALU.subtract, ALU.mult))
            dve.wait_ge(acol_in, 16)
            v.tensor_scalar(ac16[:, :], a_col, used32[:, 0:1], last32[:, 0:1], ALU.mult, ALU.add).then_inc(ac_ok, 1)
            agg_low(7)
            dve.wait_ge(kb_ok, 1)
            for t in range(DT):
                last = v.scalar_tensor_tensor(qk[:, t, :], psum[:, 2, t * HALF:(t + 1) * HALF], bqk[:, 0, t:t + 1],
                                              kb[:, t, :], ALU.add, ALU.mult)
            last.then_inc(qk_ok, 1)
            dve.wait_ge(sT_ps, 1)
            scores = psum[:, 3, :].rearrange("p (h s) -> p h s", s=HALF)
            did.did(v.tensor_tensor(sI[:, :, :], scores, same[:, None, :].to_broadcast([P, HEADS, HALF]), ALU.mult))
            v.tensor_tensor(sT[:, :, :], scores, rowm[:, None, 0:HALF].to_broadcast([P, HEADS, HALF]),
                            ALU.mult).then_inc(sT_used, 1)
            dve.wait_ge(sT_used, 1)
            link(v.tensor_tensor(sT[:, :, :], sT[:, :, :], rowoff[:, None, :].to_broadcast([P, HEADS, HALF]), ALU.add))
            did.did(v.tensor_reduce(mx[:, :], sT[:, :, :], AX.X, ALU.max))
            link(v.tensor_reduce(arg[:, 0, :], sI[:, :, :], AX.X, ALU.add))
            link(v.tensor_scalar(mx[:, :], mx[:, :], DIAG, None, ALU.max))
            did.did(v.tensor_scalar(arg[:, 1, :], mx[:, :], -1.0, None, ALU.mult))
            did.did(v.tensor_scalar(arg[:, 2, :], mx[:, :], -1.0, DIAG, ALU.mult, ALU.add))
            link(v.tensor_tensor(arg[:, 0, :], arg[:, 0, :], mx[:, :], ALU.subtract))
            v.tensor_scalar(arg[:, 0, :], arg[:, 0, :], 0.0, None, ALU.min).then_inc(arg_ok, 1)
            agg_low(8)
            dve.wait_ge(ex_ok, 1)
            v.tensor_scalar(exu[:, 0:HEADS], ex[:, 0, :], ul[:, 0:1], None, ALU.mult).then_inc(exu_ok, 1)
            dve.wait_ge(zz_ps, 1)
            link(v.tensor_scalar(nn[:, :], zs[:, ZDEG:ZDEG + 1], 1.0, psum[:, 2, HEADS:HEADS + 1],
                                 ALU.subtract, ALU.subtract))
            link(v.scalar_tensor_tensor(zz[:, :], ex[:, 1, :], nn[:, 0:1], ex[:, 2, :], ALU.mult, ALU.add))
            link(v.tensor_tensor(zz[:, :], zz[:, :], psum[:, 2, 0:HEADS], ALU.add))
            link(v.reciprocal(zz[:, :], zz[:, :]))
            did.did(v.tensor_tensor(arg[:, 0:2, :], ex[:, 1:3, :], zz[:, None, :].to_broadcast([P, 2, HEADS]), ALU.mult))
            link(v.tensor_tensor(arg[:, 2, :], exu[:, 0:HEADS], zz[:, :], ALU.mult))
            link(v.tensor_reduce(cdw[:, :], arg[:, :, :], AX.X, ALU.add))
            link(v.tensor_scalar(cdw[:, :], cdw[:, :], 1.0 / HEADS, None, ALU.mult))
            link(v.scalar_tensor_tensor(sm[:, 0:1], cdw[:, 0:1], ul[:, 0:1], cdw[:, 2:3], ALU.mult, ALU.subtract))
            v.tensor_scalar(xoc, xo[0:HALF, :], sm[0:HALF, 0:1], -1.0, ALU.mult, ALU.mult).then_inc(xoc_ok, 1)
            did.did(v.tensor_tensor(sm[:, 1:2], cdw[:, 1:2], cdw[:, 0:1], ALU.subtract))
            link(v.tensor_scalar(sm[:, 2:3], cdw[:, 0:1], sm[:, 4:5], 1.0 / ALPHA, ALU.mult, ALU.mult))
            did.did(v.tensor_scalar(sm[:, 1:2], sm[:, 1:2], XS, XS, ALU.mult, ALU.add))
            link(v.tensor_tensor(sm[:, 3:4], sm[:, 2:3], sm[:, 6:7], ALU.mult))
            v.tensor_tensor(sm[:, 3:4], sm[:, 1:2], sm[:, 3:4], ALU.subtract).then_inc(coefe_ok, 1)
            dve.wait_ge(txe_ok, 1)
            link(v.scalar_tensor_tensor(ze[:, 0, :], zs[:, 0:D], sm[:, 2:3], txe, ALU.mult, ALU.add))
            dve.wait_ge(corr_ps, 1)
            link(v.scalar_tensor_tensor(ze[:, 0, :], psum[:, 3, :], XS, ze[:, 0, :], ALU.mult, ALU.add))
            link(v.bn_stats(ste[:, :], ze[:, 0, :]))
            v.bn_aggr(mve[:, :], ste[:, :]).then_inc(ze_ok, 1)
            dve.wait_ge(sde_ok, 1)
            link(v.reciprocal(rse[:, :], sde[:, :]))
            link(v.tensor_scalar(rse[:, :], rse[:, :], ul[:, 1:2], None, ALU.mult))
            link(v.tensor_scalar(ze[:, 0, :], ze[:, 0, :], mve[:, 0:1], rse[:, 0:1], ALU.subtract, ALU.mult))
            v.tensor_tensor(delta, ze[:, 0, :], ze[:, 1, :], ALU.subtract).then_inc(delta_ok, 1)
            dve.wait_ge(delta_ok, 1)
            did.did(v.tensor_copy(d16[0:HALF, :], delta[0:HALF, :]))
            link(v.tensor_copy(hi_tmp[HALF:P, 0, :], delta[HALF:P, :]))
            v.tensor_tensor(d16[HALF:P, :], delta[HALF:P, :], hi_tmp[HALF:P, 0, :], ALU.subtract).then_inc(d16_ok, 1)
            agg_low(9)
            agg_low(10)
            agg_low(11)
            dve.wait_ge(dT_hi, 1)
            v.tensor_tensor(dT16[:, 1, :, :].rearrange("p t n -> p (t n)"), psum[:, 2, :],
                            dT16[:, 0, :, :].rearrange("p t n -> p (t n)"), ALU.subtract).then_inc(dT_lo, 1)
            dve.wait_ge(dw_ps, 1)
            v.scalar_tensor_tensor(vv[:, :], psum[:, 3, :], 1.0 / XS, bt[:, :], ALU.mult, ALU.add).then_inc(v_ok, 1)
            dve.wait_ge(v_ok, 1)
            did.did(v.tensor_copy(v16[0:HALF, :], vv[0:HALF, :]))
            link(v.tensor_copy(hi_tmp[HALF:P, 1, :], vv[HALF:P, :]))
            v.tensor_tensor(v16[HALF:P, :], vv[HALF:P, :], hi_tmp[HALF:P, 1, :], ALU.subtract).then_inc(v16_ok, 1)

            def limits():
                dve.wait_ge(checks, 1)
                dve.wait_ge(adj_checked, KT)
                dve.wait_ge(vsq_ok, 1)
                did.did(v.tensor_copy(seen[:, 4:5], before[:, :]))
                did.did(v.tensor_reduce(seen[:, 0:1], adj_off[:, :], AX.X, ALU.add))
                did.did(v.tensor_reduce(seen[:, 1:2], x_sq[:, :], AX.X, ALU.max))
                link(v.tensor_reduce(seen[:, 3:4], deg[:, :], AX.X, ALU.max))
                link(v.tensor_tensor(kept[:, :], seen[:, :], limit[:, :], ALU.is_le))
                link(v.tensor_reduce(kept1[:, :], kept[:, :], AX.X, ALU.min))
                v.tensor_copy(kept16[:, :], kept1[:, :]).then_inc(kept_ok, 1)

            def flag_out():
                dve.wait_ge(kept_ps, 1)
                v.tensor_scalar(flag[0:1, 0:1], psum[0:1, 3, 0:1], P - 0.5, None, ALU.is_lt).then_inc(flag_ok, 1)
                dve.wait_ge(flag_ok, 1)

            def finish2(i):
                r = krows(i)
                dve.wait_ge(sd2_ok, i + 1)
                link(v.reciprocal(rs[0:r, i % 4:i % 4 + 1], sd[0:r, i % 4:i % 4 + 1]))
                if i == KT - 1:
                    dve.wait_ge(out_done[i % 3], 16 * (i // 3))
                    v.tensor_scalar(y[0:r, i % 3, :], z[0:r, i % ZB, 0:D], z[0:r, i % ZB, ZMEAN:ZMEAN + 1],
                                    rs[0:r, i % 4:i % 4 + 1], ALU.subtract, ALU.mult).then_inc(bias_ok, 1)
                    return
                v.tensor_scalar(nb[0:r, i % 4:i % 4 + 1], z[0:r, i % ZB, ZMEAN:ZMEAN + 1], rs[0:r, i % 4:i % 4 + 1], -1.0,
                                ALU.mult, ALU.mult).then_inc(bias_ok, 1)

            for i in range(KT):
                r = krows(i)
                dve.wait_ge(y_ps, i + 1)
                dve.wait_ge(x2_fixed, i + 1)
                if i >= ZB:
                    dve.wait_ge(y_ok, i - ZB + 1)
                if i < KT - 1:
                    v.scalar_tensor_tensor(z[0:r, i % ZB, 0:D], psum[0:r, Y_BANK[i], :], 0.0, x2[0:r, i, :],
                                           ALU.max, ALU.add).then_inc(y_used, 1)
                    statistics(r, i, var2_ok, (y_used, i + 1))
                else:
                    for n, (c0, c1) in enumerate(PARTS):
                        dve.wait_ge(y_ps, KT + n)
                        v.scalar_tensor_tensor(z[0:r, i % ZB, c0:c1], psum[0:r, PART_BANK[n], 0:c1 - c0], 0.0,
                                               x2[0:r, i, c0:c1], ALU.max, ALU.add).then_inc(y_used, 1)
                        dve.wait_ge(y_used, KT + n)
                        did.did(v.bn_stats(st[0:r, 2 + n, :], z[0:r, i % ZB, c0:c1]))
                    did.wait(dve)
                    v.bn_aggr(z[0:r, i % ZB, ZMEAN:ZVAR + 1], st[0:r, 2:4, :]).then_inc(var2_ok, 1)
                if i >= 1:
                    finish2(i - 1)
                if i == 2:
                    limits()
                if i == 9:
                    flag_out()
            finish2(KT - 1)

        @block.tensor
        def _(pe):
            mm = nc.tensor.matmul

            def layer_one(i, k, halves=range(2)):
                m, r = krows(i), krows(k)
                for h in halves:
                    last = mm(psum[0:m, L0_BANK[i], :], a16[0:r, k, i * P:i * P + m], x16[0:r, h, k, :],
                              start=(k == 0 and h == 0), stop=(k == KT - 1 and h == 1))
                return last

            pe.wait_ge(ones_ok, 1)
            for n in range(WARM):
                mm(psum[:, DEG_BANK, :], warm[:, 0:P], warm, start=True, stop=True)
            pe.wait_ge(x_hi, 1)
            for n, (c0, c1) in enumerate(FIRST):
                pe.wait_ge(a16_first, n + 1)
                for h in range(2):
                    if h == 1:
                        pe.wait_ge(x_lo, 1)
                    for i in range(c0 // P, c1 // P):
                        layer_one(i, 0, (h,))
            for k in range(1, KT):
                pe.wait_ge(a16_ok, k + 1)
                pe.wait_ge(x_lo, k + 1)
                for i in range(G1):
                    last = layer_one(i, k)
                    if k == KT - 1:
                        last.then_inc(l0_ps, 1)
            pe.wait_ge(ones_ok, 2)
            pe.wait_ge(sum_ok, KT - 1)
            for i in range(KT):
                last = mm(psum[0:krows(i), DEG_BANK, i:i + 1], a_sum[:, i * P:i * P + krows(i)], ones1[:, 0:1],
                          start=True, stop=True)
            last.then_inc(deg_ps, 1)
            for i in range(G1, KT):
                if i > G1:
                    pe.wait_ge(z_ok, i - G1)
                for k in range(KT):
                    last = layer_one(i, k)
                last.then_inc(l0_ps, 1)

            def layer_two(n, k):
                t, c = BLOCKS[n]
                c0, w = CHUNKS[c]
                r = krows(k)
                for h in range(2):
                    last = mm(psum[:, A_BANK[n % 6], 0:w], x216[0:r, h, k, t * P:(t + 1) * P], a16[0:r, k, c0:c0 + w],
                              start=(k == 0 and h == 0), stop=(k == KT - 1 and h == 1))
                return last

            def prefix(n):
                pe.wait_ge(total_ok, n + 1)
                if n:
                    pe.wait_ge(one_ok, n)
                else:
                    pe.wait_ge(const_in, 32)
                mm(psum[0:EP, 2, 0:1], tri, total16[:, :], start=True, stop=True)
                mm(psum[:, 2, 1:2], ones16[0:EP, :], total16[:, :], start=True, stop=True).then_inc(off_ps, 1)

            def fill_slots(n):
                pe.wait_ge(one_ok, n + 1)
                for c in range(*BATCHES[n]):
                    last = mm(psum[0:HALF, 3, 0:3], one_slot[:, c, :], vals[:, c, :], start=(c == 0), stop=(c == EC - 1))
                return last

            for first, end, some in ((0, CATCH_UP, range(4)), (0, CATCH_UP, range(4, G1)), (CATCH_UP, KT, range(G1))):
                for k in range(first, end):
                    pe.wait_ge(x2_lo, k + 1)
                    if k == PREFIX_AT:
                        pe.wait_ge(z_ok, KT)
                        prefix(0)
                    if k == KT - 1:
                        fill_slots(0)
                    for n in some:
                        if k == 0:
                            pe.wait_ge(z_ok, {4: 5, 5: 6, 6: 6, 7: 7, 0: 8, 1: 9}[A_BANK[n]])
                        last = layer_two(n, k)
                        if k == KT - 1:
                            last.then_inc(agg_ps, 1)

            STEPS = [(n, k) for n in range(G1, 2 * G1) for k in range(KT)]

            def blocks(first, end):
                for n, k in STEPS[first:end]:
                    if k == 0:
                        pe.wait_ge(agg_lo, n - G1 + 1)
                    last = layer_two(n, k)
                    if k == KT - 1:
                        last.then_inc(agg_ps, 1)

            a = AT
            blocks(0, a[0])
            prefix(1)
            blocks(a[0], a[1])
            fill_slots(1)
            prefix(2)
            blocks(a[1], a[2])
            fill_slots(2).then_inc(slot_ps, 1)
            blocks(a[2], a[3])
            pe.wait_ge(slot_ok, 1)
            mm(psum[:, 2, 0:384], ones16[0:HALF, :], spread[:, :, :].rearrange("p t s -> p (t s)"),
               start=True, stop=True)
            mm(psum[:, 2, 384:387], twice16, slot16[:, :], start=True, stop=True).then_inc(across_ps, 1)
            blocks(a[3], a[4])
            pe.wait_ge(xs_in, 16)
            pe.wait_ge(xo_in, 16)
            for n, t_rows in enumerate((xs, xo)):
                for t in range(DT):
                    last = nc.tensor.transpose(psum[:, 3, (n * DT + t) * HALF:(n * DT + t + 1) * HALF],
                                               t_rows[0:HALF, t * P:(t + 1) * P], ident[0:HALF, 0:HALF])
            last.then_inc(xsoT_ps, 1)
            blocks(a[4], a[5])
            pe.wait_ge(xsoT_ok, 1)
            pe.wait_ge(wqk_in, 32)
            pe.wait_ge(rowm_ok, 1)
            for w in range(2):
                for to in range(DT):
                    for t in range(DT):
                        last = mm(psum[:, 2, (w * DT + to) * HALF:(w * DT + to + 1) * HALF],
                                  wqk[:, w, t, to * P:(to + 1) * P], xsoT[:, w * DT + t, :],
                                  start=(t == 0), stop=(t == DT - 1))
            last.then_inc(qk_ps, 1)
            blocks(a[5], a[6])
            pe.wait_ge(qk_ok, 1)
            for odd in range(2):
                last = mm(psum[:, 3, odd * DT * HALF:(odd + 1) * DT * HALF], hsel[:, odd, :],
                          qk[:, :, :].rearrange("p t s -> p (t s)"), start=True, stop=True)
            last.then_inc(sT_ps, 1)
            blocks(a[6], a[7])
            pe.wait_ge(exu_ok, 1)
            mm(psum[:, 2, 0:HEADS + 1], rowm[0:HALF, :], exu[0:HALF, :], start=True, stop=True).then_inc(zz_ps, 1)
            blocks(a[7], a[8])
            pe.wait_ge(xoc_ok, 1)
            mm(psum[:, 3, :], rowm[0:HALF, :], xoc, start=True, stop=True).then_inc(corr_ps, 1)
            blocks(a[8], len(STEPS))

            def out_tile(i):
                if i < KT - 1:
                    m = krows(i)
                    if i < G1:
                        pe.wait_ge(agg_lo, max(8 + 2 * (i * P // 512), G1 + i + 1))
                    else:
                        pe.wait_ge(y_used, i - G1 + 1)
                    if i == 8:
                        pe.wait_ge(agg_lo, 12)
                    for t in range(DT):
                        for h, hw in ((0, 0), (0, 1), (1, 0)):
                            mm(psum[0:m, Y_BANK[i], :], agg16[:, h, t, i * P:i * P + m], w16[:, hw, t, :],
                               start=(t == 0 and (h, hw) == (0, 0)), stop=False)

            def difference(i):
                if i < KT:
                    m = krows(i)
                    if i >= 2:
                        pe.wait_ge(r_copied, i - 1)
                    mm(psum[0:m, R_BANK[i], :], oh16[:, i * P:i * P + m], d16, start=True, stop=True).then_inc(r_ps, 1)

            def transpose_delta():
                pe.wait_ge(delta_ok, 1)
                for t in range(DT):
                    last = nc.tensor.transpose(psum[:, 2, t * P:(t + 1) * P], delta[:, t * P:(t + 1) * P], ident)
                last.then_inc(dT_ps, 1)

            pe.wait_ge(w_lo, 1)
            out_tile(0)
            transpose_delta()
            out_tile(1)
            pe.wait_ge(dT_lo, 1)
            for t in range(DT):
                for h, hw in ((0, 0), (0, 1), (1, 0)):
                    last = mm(psum[:, 3, :], dT16[:, h, t, :], w16[:, hw, t, :],
                              start=(t == 0 and (h, hw) == (0, 0)), stop=(t == DT - 1 and h == 1))
            last.then_inc(dw_ps, 1)
            pe.wait_ge(d16_ok, 1)
            pe.wait_ge(oh_ok, 1)
            difference(0)
            out_tile(2)
            pe.wait_ge(v_ok, 1)
            difference(1)
            pe.wait_ge(v16_ok, 1)
            pe.wait_ge(ac_ok, 1)
            tile = 3
            for i in range(KT):
                m = krows(i)
                if i < KT - 1:
                    mm(psum[0:m, Y_BANK[i], :], ac16[:, i * P:i * P + m], v16[:, :],
                       start=False, stop=True).then_inc(y_ps, 1)
                else:
                    for n, (c0, c1) in enumerate(PARTS):
                        pe.wait_ge(y_used, KT - G1 + n)
                        for t in range(DT):
                            for h, hw in ((0, 0), (0, 1), (1, 0)):
                                mm(psum[0:m, PART_BANK[n], 0:c1 - c0], agg16[:, h, t, i * P:i * P + m],
                                   w16[:, hw, t, c0:c1], start=(t == 0 and (h, hw) == (0, 0)), stop=False)
                        mm(psum[0:m, PART_BANK[n], 0:c1 - c0], ac16[:, i * P:i * P + m], v16[:, c0:c1],
                           start=False, stop=True).then_inc(y_ps, 1)
                difference(i + 2)
                if i not in CLOSE_UP:
                    out_tile(tile)
                    tile += 1
                if i == KT - 3:
                    pe.wait_ge(kept_ok, 1)
                    pe.wait_ge(r_copied, KT - 1)
                    mm(psum[:, 3, 0:1], ones16, kept16[:, :], start=True, stop=True).then_inc(kept_ps, 1)


def shape_constants():
    row, column = np.arange(P)[:, None], np.arange(P)[None, :]
    c32 = np.zeros((P, C32), np.float32)
    c32[:, 0:P] = row == column
    c32[:, P:P + HALF] = row % HALF == column[:, 0:HALF]
    c32[:, P + HALF:2 * P] = row % HALF > column[:, 0:HALF]
    for a in range(2):
        c32[a * HALF:(a + 1) * HALF, (2 + a) * P:(3 + a) * P] = DK ** -0.5
    c32[:, 4 * P] = AS * (np.arange(P) % HALF == SLOTS)
    c16 = np.zeros((P, C16), np.float16)
    c16[:, 0:N] = np.arange(N)
    c16[:, N:N + P] = 1
    c16[:, N + P:N + P + EP] = row < column[:, 0:EP]
    c16[:, N + P + EP:N + P + EP + HALF] = np.where(np.arange(HALF) < SLOTS, np.arange(HALF) + 1, -1)
    c16[:, N + P + EP + HALF:] = row == column % HALF
    return c32, c16

def build(nc, x, adj, pairs, bq, bk, b, diag, xT, adjT, wqT, wkT, wT, const32, const16, x2d, zrows, out):
    with ExitStack() as ctx:
        flag = ctx.enter_context(nc.sbuf_tensor("flag", [1, 1], I32))
        fast_path(nc, flag, x, adj, adjT, diag, pairs, wqT, bq, wkT, bk, wT, b, const32, const16, zrows, out)
        general_path(nc, flag, None, x, xT, adj, adjT, pairs, wqT, bq, wkT, bk, wT, b, x2d, out)


def kernel(**inputs):
    import numpy as _np
    import concourse.bacc as _bacc
    from concourse import mybir as _mybir
    from concourse.bass_utils import run_bass_kernel_spmd as _run

    nc = _bacc.Bacc("TRN2", target_bir_lowering=False, num_devices=1)
    given = {
        "x": inputs["x"], "adj": inputs["adj"], "pairs": inputs["L0_gnn_rel_pair_index"],
        "bq": inputs["L0_gnn_bq"], "bk": inputs["L0_gnn_bk"], "b": inputs["L1_gnn_b"],
        "diag": _np.diagonal(inputs["adj"]), "xT": _np.asarray(inputs["x"]).T, "adjT": _np.asarray(inputs["adj"]).T,
        "wqT": _np.asarray(inputs["L0_gnn_Wq"]).T, "wkT": _np.asarray(inputs["L0_gnn_Wk"]).T,
        "wT": _np.asarray(inputs["L1_gnn_W"]).T,
    }
    given["const32"], given["const16"] = shape_constants()
    arrays, aps = {}, {}
    for name, a in given.items():
        a = _np.ascontiguousarray(a)
        arrays["in_" + name] = a
        aps[name] = nc.dram_tensor("in_" + name, a.shape, _mybir.dt.from_np(a.dtype), kind="ExternalInput").ap()
    out = nc.dram_tensor("out", (N, D), F32, kind="ExternalOutput").ap()
    x2d = nc.dram_tensor("x2d", (N, D), F32, kind="Internal").ap()
    zrows = nc.dram_tensor("zrows", (N, ZW), F32, kind="Internal").ap()
    build(nc, x2d=x2d, zrows=zrows, out=out, **aps)
    r = _run(nc, [arrays], core_ids=[0])
    return r.results[0]["out"]
```
